# Optimizing a Trainium2 kernel written in Bass

```python
import numpy as np
import jax
import jax.numpy as jnp

def _softmax(x, axis=-1):
    return jax.nn.softmax(x, axis=axis)

def _gelu(x):
    return jax.nn.gelu(x, approximate=True)

def _silu(x):
    return jax.nn.silu(x)

def _sigmoid(x):
    return jax.nn.sigmoid(x)

def _layernorm(x, axis=-1, eps=1e-05):
    m = jnp.mean(x, axis=axis, keepdims=True)
    v = jnp.var(x, axis=axis, keepdims=True)
    return (x - m) / jnp.sqrt(v + eps)

def _scatter_add(tgt, idx, src, axis=0):
    return tgt.at[idx].add(src)

def _segment_sum(src, seg, n):
    return jax.ops.segment_sum(src, seg, n)
kernel_name = 'mk_conv_seq_d1_conv_nchw256_r4_e1305b'

def setup_inputs(seed: int=0):
    np.random.seed(seed)
    _w = jnp.asarray

    def _rec_inputs():
        import jax
        import jax.numpy as jnp
        _gk = jax.random.key(seed)
        x = -0.0002928 + 1 * jax.random.normal(jax.random.fold_in(_gk, 1), (4, 64, 16, 16), jnp.float32)
        return x
    x = _rec_inputs()

    def _L0_conv_setup():
        import jax, jax.numpy as jnp
        import numpy as np
        NUM_HEADS = 4
        NUM_GROUPS = 8
        EPS = 1e-05
        key = jax.random.key(seed)
        ks = jax.random.split(key, 4)
        B, C, H, W = (4, 64, 16, 16)
        x = jax.random.normal(ks[0], (B, C, H, W), dtype=jnp.float32)
        gn_w = jnp.ones((C,), dtype=jnp.float32)
        gn_b = jnp.zeros((C,), dtype=jnp.float32)
        w_qkv = jax.random.normal(ks[1], (3 * C, C), dtype=jnp.float32) * (1.0 / np.sqrt(C))
        b_qkv = jnp.zeros((3 * C,), dtype=jnp.float32)
        w_proj = jax.random.normal(ks[2], (C, C), dtype=jnp.float32) * (1.0 / np.sqrt(C))
        b_proj = jnp.zeros((C,), dtype=jnp.float32)
        return {'x': x, 'gn_w': gn_w, 'gn_b': gn_b, 'w_qkv': w_qkv, 'b_qkv': b_qkv, 'w_proj': w_proj, 'b_proj': b_proj}
    _L0_conv_all = _L0_conv_setup()
    _L0_conv_in = {k: v for k, v in _L0_conv_all.items() if k in ('gn_w', 'gn_b', 'w_qkv', 'b_qkv', 'w_proj', 'b_proj')}
    del _L0_conv_all
    return {'x': x, 'L0_conv_gn_w': _L0_conv_in['gn_w'], 'L0_conv_gn_b': _L0_conv_in['gn_b'], 'L0_conv_w_qkv': _L0_conv_in['w_qkv'], 'L0_conv_b_qkv': _L0_conv_in['b_qkv'], 'L0_conv_w_proj': _L0_conv_in['w_proj'], 'L0_conv_b_proj': _L0_conv_in['b_proj']}

def reference(x, L0_conv_gn_w, L0_conv_gn_b, L0_conv_w_qkv, L0_conv_b_qkv, L0_conv_w_proj, L0_conv_b_proj):
    import jax
    import jax.numpy as jnp

    def _L0_conv_ref(x, gn_w, gn_b, w_qkv, b_qkv, w_proj, b_proj):
        import jax, jax.numpy as jnp
        import numpy as np
        NUM_HEADS = 4
        NUM_GROUPS = 8
        EPS = 1e-05
        B, C, H, W = x.shape
        N = H * W
        nh = NUM_HEADS
        dh = C // nh
        xg = x.reshape(B, NUM_GROUPS, C // NUM_GROUPS, N)
        mu = jnp.mean(xg, axis=(2, 3), keepdims=True)
        var = jnp.var(xg, axis=(2, 3), keepdims=True)
        h = ((xg - mu) * jax.lax.rsqrt(var + EPS)).reshape(B, C, N)
        h = h * gn_w[None, :, None] + gn_b[None, :, None]
        qkv = jnp.einsum('oc,bcn->bon', w_qkv, h) + b_qkv[None, :, None]
        q, k, v = jnp.split(qkv, 3, axis=1)
        q = q.reshape(B, nh, dh, N)
        k = k.reshape(B, nh, dh, N)
        v = v.reshape(B, nh, dh, N)
        scores = jnp.einsum('bhdi,bhdj->bhij', q, k) / jnp.sqrt(jnp.array(dh, dtype=x.dtype))
        attn = jax.nn.softmax(scores, axis=-1)
        out = jnp.einsum('bhij,bhdj->bhdi', attn, v).reshape(B, C, N)
        out = jnp.einsum('oc,bcn->bon', w_proj, out) + b_proj[None, :, None]
        return x + out.reshape(B, C, H, W)

    def _gn(v, G=32, eps=1e-05):
        B_, C_, H_, W_ = v.shape
        g = v.reshape(B_, G, C_ // G, H_, W_)
        m = jnp.mean(g, axis=(2, 3, 4), keepdims=True)
        s = jnp.var(g, axis=(2, 3, 4), keepdims=True)
        return ((g - m) / jnp.sqrt(s + eps)).reshape(v.shape)

    def _ln_c(v, eps=1e-06):
        m = jnp.mean(v, axis=1, keepdims=True)
        s = jnp.var(v, axis=1, keepdims=True)
        return (v - m) / jnp.sqrt(s + eps)

    def _ln_t(v, eps=1e-05):
        m = jnp.mean(v, axis=-1, keepdims=True)
        s = jnp.var(v, axis=-1, keepdims=True)
        return (v - m) / jnp.sqrt(s + eps)

    def _to_tokens(v):
        B_, C_, H_, W_ = v.shape
        return v.reshape(B_, C_, H_ * W_).transpose(0, 2, 1)

    def _from_tokens(t, like):
        B_, C_, H_, W_ = like.shape
        return t.transpose(0, 2, 1).reshape(B_, C_, H_, W_)
    x = _L0_conv_ref(x, L0_conv_gn_w, L0_conv_gn_b, L0_conv_w_qkv, L0_conv_b_qkv, L0_conv_w_proj, L0_conv_b_proj)
    return x

_drawn_inputs = setup_inputs


def setup_inputs(seed=0):
    import zlib

    import numpy as np

    out = dict(_drawn_inputs(seed))
    spreads = {'L0_conv_gn_w': (1.0, 0.2),
     'L0_conv_gn_b': (0.0, 0.1),
     'L0_conv_b_qkv': (0.0, 0.1),
     'L0_conv_b_proj': (0.0, 0.1)}
    factors = {}
    for name, (base, spread) in spreads.items():
        noise = np.random.default_rng([zlib.crc32(name.encode()), seed]).standard_normal(out[name].shape)
        drawn = base * np.exp(spread * noise) if base else spread * noise
        out[name] = jnp.asarray(drawn.astype(out[name].dtype))
    for name, factor in factors.items():
        out[name] = (out[name] * factor).astype(out[name].dtype)
    return out
```

```python
from contextlib import ExitStack

import concourse.bass as bass
from concourse import mybir

ALU = mybir.AluOpType
ACT = mybir.ActivationFunctionType
AX_X = mybir.AxisListType.X
F32 = mybir.dt.float32
F16 = mybir.dt.float16


def groupnorm_attention(
    nc: bass.Bass,
    x: bass.AP,
    gn_w: bass.AP,
    gn_b: bass.AP,
    w_qkv: bass.AP,
    b_qkv: bass.AP,
    w_proj: bass.AP,
    b_proj: bass.AP,
    out: bass.AP,
):
    P = 128
    B, C, HH, WW = x.shape
    N = HH * WW
    NH = 4
    D = C // NH
    GROUPS = 8
    GC = C // GROUPS
    EPS = 1e-5
    SCALE = 1.0 / float(D) ** 0.5
    T = B // 2
    NT = N // P
    Q = P // NH
    MS = 64.0
    RS = 2
    RT = 2
    RP = 8
    assert C * 2 == P and D * 2 == Q and N == 2 * P and B == 4

    x_v = x.rearrange("(t p) c h w -> (p c) t (h w)", p=2)
    out_v = out.rearrange("(t p) c h w -> (p c) t (h w)", p=2)
    WR = 3 * C // 2

    with ExitStack() as ctx:
        def sb(name, shape, dt):
            return ctx.enter_context(nc.sbuf_tensor(name, shape, dt))

        def psum(name, cols):
            return ctx.enter_context(nc.psum_tensor(name, [P, cols], F32))

        def sem(name):
            return ctx.enter_context(nc.semaphore(name))

        x_sb = sb("x_sb", [P, T, N], F32)
        w_rows = sb("w_rows", [WR, 2, C], F32)
        w_dup = sb("w_dup", [WR, 2, 2, C], F32)
        wp_rows = sb("wp_rows", [C, C], F32)
        vec_rows = sb("vec_rows", [6, C], F32)
        vec_dup = sb("vec_dup", [6, 2, P], F32)
        ident = sb("ident", [P, P], F32)
        ident16 = sb("ident16", [P, P], F16)
        first16 = sb("first16", [P, P], F16)
        group_avg = sb("group_avg", [P, P], F32)
        minus_half = sb("minus_half", [P, T], F32)
        half_cols = sb("half_cols", [P, NH], F32)
        vec_h = sb("vec_h", [P, 6], F32)
        vec_c = sb("vec_c", [P, 6], F32)
        kb = sb("kb", [P, 2], F32)
        w16 = sb("w16", [P, 2, 5 * C], F16)
        wp_t = sb("wp_t", [C, C], F32)
        bn = sb("bn", [P, T, 6], F32)
        mv = sb("mv", [P, T, 2], F32)
        st = sb("st", [P, T, 2], F32)
        gst = sb("gst", [P, T, 2], F32)
        msq = sb("msq", [P, T], F32)
        ve = sb("ve", [P, T], F32)
        rstd = sb("rstd", [P, T], F32)
        ga = sb("ga", [P, T], F32)
        gb = sb("gb", [P, T], F32)
        hn = sb("hn", [P, T, N], F32)
        h16 = sb("h16", [P, B, N], F16)
        q_hi = sb("q_hi", [P, B, N], F16)
        q_lo = sb("q_lo", [P, B, N], F16)
        q_lom = sb("q_lom", [P, B, N], F16)
        k_hi2 = sb("k_hi2", [P, N], F16)
        k_all = sb("k_all", [P, B, 2, N], F16)
        k_head = sb("k_head", [P, 2, NH, 2, N], F16)
        v_sb = sb("v_sb", [P, B, NT, NH, Q], F32)
        mx = sb("mx", [P, B, NT, NH], F32)
        m_cols = sb("m_cols", [P, 2, NT, P], F16)
        probs = sb("probs", [P, RP, NT * N], F32)
        o_sb = sb("o_sb", [P, B, N], F32)
        rden = sb("rden", [P, B, NT * NH], F32)
        o_n = sb("o_n", [P, B, NT * NH, D], F32)
        ont_sb = sb("ont_sb", [C, B, N], F32)
        y_sb = sb("y_sb", [P, T, N], F32)

        ps_s = psum("ps_s", RS * 512)
        ps_t = psum("ps_t", RT * 512)
        ps_q = psum("ps_q", 512)
        ps_km = psum("ps_km", 512)
        ps_o = psum("ps_o", 512)
        ps_y = psum("ps_y", 512)

        x_in = [sem(f"x_in{t}") for t in range(T)]
        wqkv_in = sem("wqkv_in")
        wproj_in = sem("wproj_in")
        vec_in = sem("vec_in")
        ident_set = sem("ident_set")
        const_set = sem("const_set")
        pool_chain = sem("pool_chain")
        zeros_set = sem("zeros_set")
        dve_chain = sem("dve_chain")
        dup_set = sem("dup_set")
        wt_done = sem("wt_done")
        vt_done = sem("vt_done")
        vec_set = sem("vec_set")
        w16_set = sem("w16_set")
        st_set = sem("st_set")
        gst_done = sem("gst_done")
        ve_set = sem("ve_set")
        rstd_set = sem("rstd_set")
        hn_set = sem("hn_set")
        hhi_set = sem("hhi_set")
        h16_set = sem("h16_set")
        qk_done = sem("qk_done")
        qhi_set = sem("qhi_set")
        k2_set = sem("k2_set")
        qlo_set = sem("qlo_set")
        k1_set = sem("k1_set")
        khead_set = sem("khead_set")
        v_done = sem("v_done")
        v_set = sem("v_set")
        s_done = sem("s_done")
        max_done = sem("max_done")
        mcols_set = sem("mcols_set")
        m_done = sem("m_done")
        qlom_set = sem("qlom_set")
        t_done = sem("t_done")
        exp_done = sem("exp_done")
        pv_done = sem("pv_done")
        o_set = sem("o_set")
        ot_done = sem("ot_done")
        on_set = sem("on_set")
        ont_done = sem("ont_done")
        ont_set = sem("ont_set")
        y_done = sem("y_done")
        y_set = sem("y_set")
        out_done = sem("out_done")

        def half(b):
            return slice((b % 2) * C, (b % 2) * C + C)

        def quad(h):
            return slice(h * Q, h * Q + Q)

        block = ctx.enter_context(nc.Block())

        @block.sync
        def _(sp):
            sp.dma_start(x_sb[:, 0, :], x_v[:, 0, :]).then_inc(x_in[0], 16)
            sp.dma_start(w_rows[:], w_qkv.rearrange("(t p) c -> p t c", t=2)).then_inc(wqkv_in, 16)
            sp.dma_start(x_sb[:, 1, :], x_v[:, 1, :]).then_inc(x_in[1], 16)
            sp.dma_start(wp_rows[:], w_proj).then_inc(wproj_in, 16)
            for b in range(B):
                sp.wait_ge(y_set, b + 1)
                sp.dma_start(out_v[half(b), b // 2, :], y_sb[half(b), b // 2, :]).then_inc(out_done, 16)
            sp.wait_ge(out_done, 16 * B)

        @block.gpsimd
        def _(pool):
            n = [0]

            def link(ins):
                n[0] += 1
                ins.then_inc(pool_chain, 1)
                pool.wait_ge(pool_chain, n[0])

            row = lambda v: v.rearrange("(a c) -> a c", a=1)
            pool.dma_start(vec_rows[3:4, :], row(gn_w)).then_inc(vec_in, 16)
            pool.dma_start(vec_rows[4:5, :], row(gn_b)).then_inc(vec_in, 16)
            pool.dma_start(vec_rows[0:3, :], b_qkv.rearrange("(a c) -> a c", a=3)).then_inc(vec_in, 16)
            pool.dma_start(vec_rows[5:6, :], row(b_proj)).then_inc(vec_in, 16)
            link(nc.gpsimd.memset(ident[:], 0.0))
            nc.gpsimd.affine_select(out=ident[:], in_=ident[:], compare_op=ALU.not_equal, fill=1.0, base=0,
                                    pattern=[[-1, P]], channel_multiplier=1).then_inc(ident_set, 1)
            link(nc.gpsimd.memset(group_avg[:], 1.0 / GC))
            ga_v = group_avg[:].rearrange("p (g c) -> p g c", c=GC)
            link(nc.gpsimd.affine_select(out=ga_v, in_=ga_v, compare_op=ALU.is_ge, fill=0.0, base=0,
                                         pattern=[[-GC, P // GC], [0, GC]], channel_multiplier=1))
            link(nc.gpsimd.affine_select(out=ga_v, in_=ga_v, compare_op=ALU.is_ge, fill=0.0, base=GC - 1,
                                         pattern=[[GC, P // GC], [0, GC]], channel_multiplier=-1))
            nc.gpsimd.memset(minus_half[:], -0.5).then_inc(const_set, 1)
            for t in range(T):
                pool.wait_ge(ve_set, t + 1)
                nc.gpsimd.tensor_tensor(rstd[:, t:t + 1], ve[:, t:t + 1], minus_half[:, t:t + 1],
                                        ALU.pow).then_inc(rstd_set, 1)
            nc.gpsimd.memset(k_head[:].rearrange("p a h b n -> p (a h b n)").bitcast(F32), 0.0).then_inc(zeros_set, 1)
            nc.gpsimd.memset(m_cols[:].rearrange("p a t n -> p (a t n)").bitcast(F32), 0.0).then_inc(zeros_set, 1)
            nc.gpsimd.memset(v_sb[:].rearrange("p b t h e -> p (b t h) e")[:, :, D:Q], 1.0).then_inc(zeros_set, 1)

        @block.tensor
        def _(pe):
            def scores(b, h):
                u = b * NH + h
                pe.wait_ge(khead_set, u + 1)
                pe.wait_ge(qhi_set, b + 1)
                if u >= RS:
                    pe.wait_ge(max_done, u - RS + 1)
                for qt in range(NT):
                    r = (u % RS) * 512 + qt * N
                    mm = nc.tensor.matmul(ps_s[:, r:r + N], q_hi[:, b, qt * P:qt * P + P], k_head[:, b % 2, h, 0, :],
                                          start=True, stop=True)
                mm.then_inc(s_done, 1)

            def scores_t(b, h):
                u = b * NH + h
                if h == 0:
                    pe.wait_ge(qlom_set, b + 1)
                if u >= RT:
                    pe.wait_ge(exp_done, u - RT + 1)
                for kt in range(NT):
                    r = (u % RT) * 512 + kt * N
                    ks = slice(kt * P, kt * P + P)
                    nc.tensor.matmul(ps_t[:, r:r + N], k_head[:, b % 2, h, 0, ks], q_hi[:, b, :],
                                     start=True, stop=False)
                    mm = nc.tensor.matmul(ps_t[:, r:r + N], k_head[:, b % 2, h, 1, ks], q_lom[:, b, :],
                                          start=False, stop=True)
                mm.then_inc(t_done, 1)

            def qk_proj(b):
                pe.wait_ge(h16_set, b + 1)
                if b == 0:
                    pe.wait_ge(w16_set, 4)
                if b >= 1:
                    pe.wait_ge(qlo_set, b)
                    pe.wait_ge(k1_set, b)
                if b >= 2:
                    pe.wait_ge(qlom_set, b - 1)
                for j, dst in enumerate((ps_q[:, 0:N], ps_km[:, N:2 * N])):
                    for part in range(2):
                        mm = nc.tensor.matmul(dst, w16[:, part, j * P:j * P + P], h16[:, b, :],
                                              start=(part == 0), stop=(part == 1))
                mm.then_inc(qk_done, 1)

            def v_proj(b):
                pe.wait_ge(h16_set, b + 1)
                for kt in range(NT):
                    for part in range(2):
                        r = (b * NT + kt) * C
                        mm = nc.tensor.matmul(ps_o[:, r:r + C], h16[:, b, kt * P:kt * P + P], w16[:, part, 2 * P:2 * P + C],
                                              start=(part == 0), stop=(part == 1))
                if b == B - 1:
                    mm.then_inc(v_done, 1)

            def max_rows(b):
                pe.wait_ge(qlo_set, b + 1)
                if b >= 1:
                    pe.wait_ge(qlom_set, b)
                pe.wait_ge(k1_set, min(b + 2, B))
                pe.wait_ge(mcols_set, b + 1)
                for qt in range(NT):
                    qs = slice(qt * P, qt * P + P)
                    nc.tensor.matmul(ps_km[:, qs], first16[:], q_lo[:, b, qs], start=True, stop=False)
                    mm = nc.tensor.matmul(ps_km[:, qs], m_cols[:, b % 2, qt, :], ident16[:], start=False, stop=True)
                mm.then_inc(m_done, 1)

            def weighted_values(b):
                pe.wait_ge(exp_done, (b + 1) * NH)
                if b == 0:
                    pe.wait_ge(v_set, 1)
                if b >= 1:
                    pe.wait_ge(o_set, b)
                for kt in range(NT):
                    for h in range(NH):
                        mm = nc.tensor.matmul(ps_o[quad(h), 0:N], v_sb[:, b, kt, h, :],
                                              probs[:, (b * NH + h) % RP, kt * N:kt * N + N],
                                              start=(kt == 0), stop=(kt == NT - 1), skip_group_check=True)
                mm.then_inc(pv_done, 1)

            def turn_out(b):
                pe.wait_ge(o_set, b + 1)
                if b >= 1:
                    pe.wait_ge(y_set, b)
                for qt in range(NT):
                    mm = nc.tensor.transpose(ps_y[:, qt * P:qt * P + P], o_sb[:, b, qt * P:qt * P + P], ident[:])
                mm.then_inc(ot_done, 1)

            def turn_back(b):
                pe.wait_ge(on_set, b + 1)
                for qt in range(NT):
                    mm = nc.tensor.transpose(ps_y[0:C, N + qt * P:N + qt * P + P],
                                             o_n[:, b, qt * NH:qt * NH + NH, :].rearrange("p h d -> p (h d)"), ident[:])
                mm.then_inc(ont_done, 1)

            def project(b):
                pe.wait_ge(ont_set, b + 1)
                nc.tensor.matmul(ps_y[half(b), 0:N], wp_t[:], ont_sb[:, b, :], start=True, stop=True).then_inc(y_done, 1)

            pe.wait_ge(ident_set, 1)
            pe.wait_ge(dup_set, 3)
            for t in range(2):
                mm = nc.tensor.transpose(ps_q[:, t * WR:t * WR + WR],
                                         w_dup[:, t, :, :].rearrange("p a c -> p (a c)"), ident[0:WR, 0:WR])
            mm.then_inc(wt_done, 1)
            for j in range(2):
                nc.tensor.transpose(ps_km[:, j * 6:j * 6 + 6], vec_dup[:, j, :], ident[0:6, 0:6])
            pe.wait_ge(wproj_in, 16)
            nc.tensor.transpose(ps_km[0:C, P:P + C], wp_rows[:], ident[0:C, 0:C]).then_inc(vt_done, 1)
            pe.wait_ge(const_set, 1)
            for t in range(T):
                pe.wait_ge(st_set, t + 1)
                nc.tensor.matmul(ps_y[:, 2 * t:2 * t + 2], group_avg[:], st[:, t, :], start=True, stop=True
                                 ).then_inc(gst_done, 1)
            qk_proj(0)
            for b in range(B):
                v_proj(b)
            for s in range(B + 2):
                for h in range(NH):
                    if s < B:
                        scores(s, h)
                    if 1 <= s <= B:
                        scores_t(s - 1, h)
                    if h == 0 and s + 1 < B:
                        qk_proj(s + 1)
                    if s >= 2 and h < 3:
                        (turn_out, turn_back, project)[h](s - 2)
                if s < B:
                    max_rows(s)
                if 1 <= s <= B:
                    weighted_values(s - 1)

        @block.vector
        def _(dve):
            n = [0]

            def link(ins):
                n[0] += 1
                ins.then_inc(dve_chain, 1)
                dve.wait_ge(dve_chain, n[0])

            def norm(t):
                dve.wait_ge(x_in[t], 16)
                link(nc.vector.bn_stats(bn[:, t, :], x_sb[:, t, :]))
                link(nc.vector.bn_aggr(mv[:, t, :], bn[:, t, :]))
                link(nc.vector.tensor_copy(st[:, t, 0:1], mv[:, t, 0:1]))
                nc.vector.scalar_tensor_tensor(out=st[:, t, 1:2], in0=mv[:, t, 0:1], scalar=mv[:, t, 0:1],
                                               in1=mv[:, t, 1:2], op0=ALU.mult, op1=ALU.add).then_inc(st_set, 1)
                dve.wait_ge(gst_done, t + 1)
                link(nc.vector.tensor_copy(gst[:, t, :], ps_y[:, 2 * t:2 * t + 2]))
                link(nc.vector.tensor_tensor(msq[:, t:t + 1], gst[:, t, 0:1], gst[:, t, 0:1], ALU.mult))
                nc.vector.scalar_tensor_tensor(out=ve[:, t:t + 1], in0=gst[:, t, 1:2], scalar=EPS,
                                               in1=msq[:, t:t + 1], op0=ALU.add, op1=ALU.subtract).then_inc(ve_set, 1)
                dve.wait_ge(rstd_set, t + 1)
                link(nc.vector.tensor_tensor(ga[:, t:t + 1], rstd[:, t:t + 1], vec_c[:, 3:4], ALU.mult))
                link(nc.vector.scalar_tensor_tensor(out=gb[:, t:t + 1], in0=gst[:, t, 0:1], scalar=ga[:, t:t + 1],
                                                    in1=vec_c[:, 4:5], op0=ALU.mult, op1=ALU.subtract))
                nc.vector.tensor_scalar(hn[:, t, :], x_sb[:, t, :], ga[:, t:t + 1], gb[:, t:t + 1],
                                        ALU.mult, ALU.subtract).then_inc(hn_set, 1)

            def h_low(b):
                dve.wait_ge(hn_set, b // 2 + 1)
                dve.wait_ge(hhi_set, b + 1)
                nc.vector.tensor_tensor(h16[half(b + 1), b, :], hn[half(b), b // 2, :], h16[half(b), b, :],
                                        ALU.subtract).then_inc(h16_set, 1)

            def qk_low(b):
                dve.wait_ge(qk_done, b + 1)
                dve.wait_ge(qhi_set, b + 1)
                nc.vector.scalar_tensor_tensor(out=q_lo[:, b, :], in0=ps_q[:, 0:N], scalar=vec_h[:, 0:1],
                                               in1=q_hi[:, b, :], op0=ALU.add, op1=ALU.subtract).then_inc(qlo_set, 1)
                dve.wait_ge(k2_set, b + 1)
                nc.vector.scalar_tensor_tensor(out=k_all[:, b, 0, :], in0=ps_km[:, N:2 * N], scalar=vec_h[:, 1:2],
                                               in1=k_hi2[:], op0=ALU.add, op1=ALU.subtract).then_inc(k1_set, 1)

            def k_spread(b):
                dve.wait_ge(k1_set, b + 1)
                dve.wait_ge(k2_set, b + 1)
                if b == 0:
                    dve.wait_ge(zeros_set, 3)
                for h in range(NH):
                    if b >= 2:
                        dve.wait_ge(t_done, (b - 2) * NH + h + 1)
                    nc.vector.tensor_copy(k_head[quad(h), b % 2, h, :, :], k_all[quad(h), b, :, :]).then_inc(khead_set, 1)

            def row_max(b, h):
                u = b * NH + h
                dve.wait_ge(s_done, u + 1)
                r = (u % RS) * 512
                nc.vector.tensor_reduce(mx[:, b, :, h], ps_s[:, r:r + NT * N].rearrange("p (t n) -> p t n", n=N),
                                        AX_X, ALU.max).then_inc(max_done, 1)

            def max_cols(b):
                dve.wait_ge(max_done, (b + 1) * NH)
                if b >= 2:
                    dve.wait_ge(m_done, b - 1)
                cols = m_cols[:, b % 2, :, :].rearrange("p t (h e) -> p t h e", e=Q)[:, :, :, D]
                nc.vector.tensor_scalar(cols, mx[:, b, :, :], 1.0 / MS, None, ALU.mult).then_inc(mcols_set, 1)

            def normalise(b):
                dve.wait_ge(ot_done, b + 1)
                ot = ps_y[:, 0:N].rearrange("p (g e) -> p g e", e=Q)
                link(nc.vector.reciprocal(rden[:, b, :], ot[:, :, D]))
                nc.vector.tensor_tensor(o_n[:, b, :, :], ot[:, :, 0:D],
                                        rden[:, b, :].unsqueeze(2).to_broadcast([P, NT * NH, D]),
                                        ALU.mult).then_inc(on_set, 1)

            def residual(b):
                dve.wait_ge(y_done, b + 1)
                nc.vector.scalar_tensor_tensor(out=y_sb[half(b), b // 2, :], in0=ps_y[half(b), 0:N],
                                               scalar=vec_c[half(b), 5:6], in1=x_sb[half(b), b // 2, :],
                                               op0=ALU.add, op1=ALU.add).then_inc(y_set, 1)

            dve.wait_ge(wqkv_in, 16)
            nc.vector.tensor_copy(w_dup[:], w_rows[:].unsqueeze(2).to_broadcast([WR, 2, 2, C])).then_inc(dup_set, 1)
            dve.wait_ge(vec_in, 64)
            nc.vector.tensor_copy(vec_dup[:, 0, :].rearrange("p (h r d) -> p h r d", r=2, d=D),
                                  vec_rows[:].rearrange("p (h d) -> p h d", d=D).unsqueeze(2).to_broadcast([6, NH, 2, D])
                                  ).then_inc(dup_set, 1)
            nc.vector.tensor_copy(vec_dup[:, 1, :].rearrange("p (r c) -> p r c", r=2),
                                  vec_rows[:].unsqueeze(1).to_broadcast([6, 2, C])).then_inc(dup_set, 1)
            dve.wait_ge(ident_set, 1)
            nc.vector.tensor_copy(ident16[:], ident[:]).then_inc(w16_set, 1)
            iq = ident[:].rearrange("p (h r d) -> p h r d", r=2, d=D)
            link(nc.vector.tensor_reduce(half_cols[:, 0:1], iq[:, :, 0, :], mybir.AxisListType.XY, ALU.add))
            link(nc.vector.tensor_reduce(half_cols[:, 1:2], iq[:, :, 1, :], mybir.AxisListType.XY, ALU.add))
            link(nc.vector.tensor_reduce(half_cols[:, 2:3], iq[:, :, 1, 0], AX_X, ALU.add))
            link(nc.vector.tensor_scalar(first16[:], ident[:], half_cols[:, 0:1], None, ALU.mult))
            dve.wait_ge(vt_done, 1)
            link(nc.vector.tensor_copy(vec_h[:], ps_km[:, 0:6]))
            link(nc.vector.tensor_copy(vec_c[:], ps_km[:, 6:12]))
            link(nc.vector.tensor_copy(wp_t[:], ps_km[0:C, P:P + C]))
            link(nc.vector.tensor_tensor(kb[:, 0:1], vec_h[:, 1:2], half_cols[:, 1:2], ALU.mult))
            link(nc.vector.tensor_tensor(kb[:, 1:2], vec_h[:, 1:2], half_cols[:, 0:1], ALU.mult))
            nc.vector.scalar_tensor_tensor(out=kb[:, 1:2], in0=half_cols[:, 2:3], scalar=-MS, in1=kb[:, 1:2],
                                           op0=ALU.mult, op1=ALU.add).then_inc(vec_set, 1)
            dve.wait_ge(wt_done, 1)
            wt_qk = ps_q[:, 0:2 * C].rearrange("p (g d) -> p g d", d=D).unsqueeze(2).to_broadcast([P, 2 * NH, 2, D])
            wt_v = ps_q[:, 2 * C:3 * C]
            part_qk = [w16[:, i, 0:4 * C].rearrange("p (g r d) -> p g r d", r=2, d=D) for i in range(2)]
            link(nc.vector.tensor_copy(part_qk[0], wt_qk))
            link(nc.vector.tensor_copy(w16[:, 0, 4 * C:5 * C], wt_v))
            nc.vector.tensor_tensor(part_qk[1], wt_qk, part_qk[0], ALU.subtract).then_inc(w16_set, 1)
            nc.vector.tensor_tensor(w16[:, 1, 4 * C:5 * C], wt_v, w16[:, 0, 4 * C:5 * C], ALU.subtract).then_inc(w16_set, 2)
            norm(0)
            h_low(0)
            h_low(1)
            norm(1)
            h_low(2)
            h_low(3)
            qk_low(0)
            k_spread(0)
            dve.wait_ge(v_done, 1)
            dve.wait_ge(zeros_set, 3)
            nc.vector.tensor_copy(v_sb[:].rearrange("p b t h e -> p (b t h) e")[:, :, 0:D],
                                  ps_o[:, :].rearrange("p (g d) -> p g d", d=D)).then_inc(v_set, 1)
            for s in range(B + 2):
                for h in range(NH):
                    if s < B:
                        row_max(s, h)
                    if h == 1 and s + 1 < B:
                        qk_low(s + 1)
                    if h == 2 and s + 1 < B:
                        k_spread(s + 1)
                    if s >= 2 and h in (0, 2):
                        (normalise, None, residual)[h](s - 2)
                if s < B:
                    max_cols(s)

        @block.scalar
        def _(act):
            def h_high(b):
                act.wait_ge(hn_set, b // 2 + 1)
                nc.scalar.activation(h16[half(b), b, :], hn[half(b), b // 2, :], ACT.Copy).then_inc(hhi_set, 1)

            def qk_high(b):
                act.wait_ge(qk_done, b + 1)
                nc.scalar.activation(q_hi[:, b, :], ps_q[:, 0:N], ACT.Identity, bias=vec_h[:, 0:1]).then_inc(qhi_set, 1)
                if b >= 1:
                    act.wait_ge(k1_set, b)
                nc.scalar.activation(k_hi2[:], ps_km[:, N:2 * N], ACT.Identity, bias=kb[:, 0:1],
                                     scale=half_cols[:, 1:2])
                nc.scalar.activation(k_all[:, b, 1, :], ps_km[:, N:2 * N], ACT.Identity, bias=kb[:, 1:2],
                                     scale=half_cols[:, 0:1]).then_inc(k2_set, 1)

            def soft_exp(b, h):
                u = b * NH + h
                act.wait_ge(t_done, u + 1)
                if u >= RP:
                    act.wait_ge(pv_done, (u - RP) // NH + 1)
                r = (u % RT) * 512
                nc.scalar.activation(probs[:, u % RP, :], ps_t[:, r:r + NT * N], ACT.Exp, scale=SCALE
                                     ).then_inc(exp_done, 1)

            def q_low_max(b):
                act.wait_ge(m_done, b + 1)
                nc.scalar.activation(q_lom[:, b, :], ps_km[:, 0:N], ACT.Copy).then_inc(qlom_set, 1)

            def save_out(b):
                act.wait_ge(pv_done, b + 1)
                nc.scalar.activation(o_sb[:, b, :], ps_o[:, 0:N], ACT.Copy).then_inc(o_set, 1)

            def save_turned(b):
                act.wait_ge(ont_done, b + 1)
                nc.scalar.activation(ont_sb[:, b, :], ps_y[0:C, N:2 * N], ACT.Identity, bias=bv[:, 0:1]).then_inc(ont_set, 1)

            for b in range(B):
                h_high(b)
            act.wait_ge(vec_set, 1)
            bv = vec_c[0:C, 2:3]
            qk_high(0)
            for s in range(B + 2):
                for h in range(NH):
                    if 1 <= s <= B:
                        soft_exp(s - 1, h)
                    if h == 0 and s + 1 < B:
                        qk_high(s + 1)
                    if h == 1 and s >= 2:
                        save_turned(s - 2)
                if s < B:
                    q_low_max(s)
                if 1 <= s <= B:
                    save_out(s - 1)


_INS = ['x', 'L0_conv_gn_w', 'L0_conv_gn_b', 'L0_conv_w_qkv', 'L0_conv_b_qkv', 'L0_conv_w_proj', 'L0_conv_b_proj']
_OUTS = [((4, 64, 16, 16), 'float32')]


def kernel(**inputs):
    import numpy as _np
    import concourse.bacc as _bacc
    from concourse import mybir as _mybir
    from concourse.bass_utils import run_bass_kernel_spmd as _run

    nc = _bacc.Bacc("TRN2", target_bir_lowering=False, num_devices=1)
    arrays, args = {}, []
    for name in _INS:
        a = _np.ascontiguousarray(inputs[name])
        arrays[f"in_{name}_dram"] = a
        args.append(nc.dram_tensor(f"in_{name}_dram", a.shape, _mybir.dt.from_np(a.dtype), kind="ExternalInput").ap())
    for i, (shape, dtype) in enumerate(_OUTS):
        dt = _mybir.dt.from_np(_np.dtype(dtype))
        args.append(nc.dram_tensor(f"out_{i}_dram", shape, dt, kind="ExternalOutput").ap())
    groupnorm_attention(nc, *args)
    r = _run(nc, [arrays], core_ids=[0])
    got = tuple(r.results[0][f"out_{i}_dram"] for i in range(len(_OUTS)))
    return got[0]
```

```python
from contextlib import ExitStack

import concourse.bass as bass
from concourse import mybir

ALU = mybir.AluOpType
ACT = mybir.ActivationFunctionType
AX_X = mybir.AxisListType.X
F32 = mybir.dt.float32
F16 = mybir.dt.float16


def groupnorm_attention(
    nc: bass.Bass,
    x: bass.AP,
    gn_w: bass.AP,
    gn_b: bass.AP,
    w_qkv: bass.AP,
    b_qkv: bass.AP,
    w_proj: bass.AP,
    b_proj: bass.AP,
    out: bass.AP,
):
    P = 128
    B, C, HH, WW = x.shape
    N = HH * WW
    NH = 4
    D = C // NH
    GROUPS = 8
    GC = C // GROUPS
    EPS = 1e-5
    SCALE = 1.0 / float(D) ** 0.5
    T = B // 2
    NT = N // P
    Q = P // NH
    MS = 64.0
    RS = 2
    RT = 2
    RP = 8
    assert C * 2 == P and D * 2 == Q and N == 2 * P and B == 4

    x_v = x.rearrange("(t p) c h w -> (p c) t (h w)", p=2)
    out_v = out.rearrange("(t p) c h w -> (p c) t (h w)", p=2)
    WR = 3 * C // 2

    with ExitStack() as ctx:
        def sb(name, shape, dt):
            return ctx.enter_context(nc.sbuf_tensor(name, shape, dt))

        def psum(name, cols):
            return ctx.enter_context(nc.psum_tensor(name, [P, cols], F32))

        def sem(name):
            return ctx.enter_context(nc.semaphore(name))

        x_sb = sb("x_sb", [P, T, N], F32)
        w_rows = sb("w_rows", [WR, 2, C], F32)
        wp_rows = sb("wp_rows", [C, C], F32)
        gn_rows = sb("gn_rows", [2, 2, C], F32)
        bh_rows = sb("bh_rows", [2, NH, 2, D], F32)
        bc_rows = sb("bc_rows", [2, 2, C], F32)
        ident = sb("ident", [P, P], F32)
        ident16 = sb("ident16", [P, P], F16)
        minus16 = sb("minus16", [P, P], F16)
        group_avg = sb("group_avg", [P, P], F32)
        minus_half = sb("minus_half", [P, T], F32)
        half_cols = sb("half_cols", [P, 3], F32)
        gn_c = sb("gn_c", [P, 2], F32)
        b_h = sb("b_h", [P, 2], F32)
        b_c = sb("b_c", [P, 2], F32)
        kb = sb("kb", [P, 2], F32)
        w16 = sb("w16", [P, 2, 5 * C], F16)
        wp_t = sb("wp_t", [C, C], F32)
        bn = sb("bn", [P, T, 6], F32)
        st = sb("st", [P, 3, T], F32)
        gst = sb("gst", [P, 3, T], F32)
        msq = sb("msq", [P, T], F32)
        ex = sb("ex", [P, T], F32)
        ve = sb("ve", [P, T], F32)
        rstd = sb("rstd", [P, T], F32)
        ga = sb("ga", [P, T], F32)
        mga = sb("mga", [P, T], F32)
        gb = sb("gb", [P, T], F32)
        hn = sb("hn", [P, T, N], F32)
        h16 = sb("h16", [P, B, N], F16)
        q_hi = sb("q_hi", [P, B, N], F16)
        q_lom = sb("q_lom", [P, B, N], F16)
        k_hi2 = sb("k_hi2", [P, 2, N], F16)
        k_all = sb("k_all", [P, B, 2, N], F16)
        k_head = sb("k_head", [P, B, NH, 2, N], F16)
        v_sb = sb("v_sb", [P, B, NT, NH, Q], F32)
        mx = sb("mx", [P, B, NT, NH], F32)
        m_cols = sb("m_cols", [P, 2, NT, P], F16)
        probs = sb("probs", [P, RP, NT * N], F32)
        o_sb = sb("o_sb", [P, B, N], F32)
        rden = sb("rden", [P, B, NT * NH], F32)
        o_n = sb("o_n", [P, B, NT * NH, D], F32)
        ont_sb = sb("ont_sb", [C, B, N], F32)
        y_sb = sb("y_sb", [P, T, N], F32)

        ps_s = psum("ps_s", RS * 512)
        ps_t = psum("ps_t", RT * 512)
        ps_q = [psum(f"ps_q{i}", 512) for i in range(2)]
        ps_k = psum("ps_k", 512)
        ps_o = psum("ps_o", 512)

        x_in = [sem(f"x_in{t}") for t in range(T)]
        wqkv_in = sem("wqkv_in")
        wproj_in = sem("wproj_in")
        gn_in = sem("gn_in")
        bh_in = sem("bh_in")
        bc_in = sem("bc_in")
        ident_set = sem("ident_set")
        const_set = sem("const_set")
        pool_chain = sem("pool_chain")
        zeros_set = sem("zeros_set")
        mz_set = sem("mz_set")
        ones_set = sem("ones_set")
        bh_set = sem("bh_set")
        dve_chain = sem("dve_chain")
        wt_done = sem("wt_done")
        gnt_done = sem("gnt_done")
        bt_done = sem("bt_done")
        wpt_done = sem("wpt_done")
        gnc_set = sem("gnc_set")
        bc_set = sem("bc_set")
        wp_set = sem("wp_set")
        const16_set = sem("const16_set")
        whi_set = sem("whi_set")
        w16_set = sem("w16_set")
        st_set = sem("st_set")
        gst_done = sem("gst_done")
        ve_set = sem("ve_set")
        rstd_set = sem("rstd_set")
        hn_set = sem("hn_set")
        gb_set = sem("gb_set")
        hhi_set = sem("hhi_set")
        h16_set = sem("h16_set")
        q_done = sem("q_done")
        k_done = sem("k_done")
        qhi_set = sem("qhi_set")
        k2_set = sem("k2_set")
        k1_set = sem("k1_set")
        khead_set = sem("khead_set")
        v_done = sem("v_done")
        v_set = sem("v_set")
        kd_set = [sem(f"kd_set{b}") for b in range(1, B)]
        s_done = sem("s_done")
        max_done = sem("max_done")
        mcols_set = sem("mcols_set")
        m_done = sem("m_done")
        qlom_set = sem("qlom_set")
        t_done = sem("t_done")
        exp_done = sem("exp_done")
        pv_done = sem("pv_done")
        o_set = sem("o_set")
        ot_done = sem("ot_done")
        on_set = sem("on_set")
        ont_done = sem("ont_done")
        ont_set = sem("ont_set")
        y_done = sem("y_done")
        fin_set = sem("fin_set")
        out_done = sem("out_done")

        def half(b):
            return slice((b % 2) * C, (b % 2) * C + C)

        def quad(h):
            return slice(h * Q, h * Q + Q)

        wt_qk = ps_t[:, 0:2 * C].rearrange("p (g d) -> p g d", d=D).unsqueeze(2).to_broadcast([P, 2 * NH, 2, D])
        wt_v = ps_t[:, 2 * C:3 * C]

        def w_part(part, v):
            if v:
                return w16[:, part, 4 * C:5 * C]
            return w16[:, part, 0:4 * C].rearrange("p (g r d) -> p g r d", r=2, d=D)

        block = ctx.enter_context(nc.Block())

        @block.sync
        def _(sp):
            sp.dma_start(x_sb[:, 0, :], x_v[:, 0, :]).then_inc(x_in[0], 16)
            sp.dma_start(x_sb[:, 1, :], x_v[:, 1, :]).then_inc(x_in[1], 16)
            sp.dma_start(w_rows[:], w_qkv.rearrange("(t p) c -> p t c", t=2)).then_inc(wqkv_in, 16)
            for i in range(2):
                src = b_qkv[i * C:i * C + C].rearrange("(a h d) -> a h d", a=1, h=NH)
                sp.dma_start(bh_rows[i:i + 1], src.unsqueeze(2).to_broadcast([1, NH, 2, D])).then_inc(bh_in, 16)
            sp.dma_start(wp_rows[:], w_proj).then_inc(wproj_in, 16)
            for i, src in enumerate((b_qkv[2 * C:3 * C], b_proj)):
                sp.dma_start(bc_rows[i:i + 1], src.rearrange("(a c) -> a c", a=1).unsqueeze(1).to_broadcast([1, 2, C])
                             ).then_inc(bc_in, 16)
            for b in range(1, B):
                sp.wait_ge(k1_set, b + 1)
                sp.wait_ge(k2_set, b + 1)
                sp.wait_ge(zeros_set, b)
                for h in range(NH):
                    sp.dma_start(k_head[quad(h), b, h, :, :], k_all[quad(h), b, :, :]).then_inc(kd_set[b - 1], 16)
            for t in range(T):
                sp.wait_ge(fin_set, 2 * t + 2)
                sp.dma_start(out_v[:, t, :], y_sb[:, t, :]).then_inc(out_done, 16)
            sp.wait_ge(out_done, 16 * T)

        @block.gpsimd
        def _(pool):
            n = [0]

            def link(ins):
                n[0] += 1
                ins.then_inc(pool_chain, 1)
                pool.wait_ge(pool_chain, n[0])

            for i, src in enumerate((gn_w, gn_b)):
                pool.dma_start(gn_rows[i:i + 1], src.rearrange("(a c) -> a c", a=1).unsqueeze(1).to_broadcast([1, 2, C])
                               ).then_inc(gn_in, 16)
            link(nc.gpsimd.memset(ident[:], 0.0))
            nc.gpsimd.affine_select(out=ident[:], in_=ident[:], compare_op=ALU.not_equal, fill=1.0, base=0,
                                    pattern=[[-1, P]], channel_multiplier=1).then_inc(ident_set, 1)
            link(nc.gpsimd.memset(group_avg[:], 1.0 / GC))
            ga_v = group_avg[:].rearrange("p (g c) -> p g c", c=GC)
            link(nc.gpsimd.affine_select(out=ga_v, in_=ga_v, compare_op=ALU.is_ge, fill=0.0, base=0,
                                         pattern=[[-GC, P // GC], [0, GC]], channel_multiplier=1))
            link(nc.gpsimd.affine_select(out=ga_v, in_=ga_v, compare_op=ALU.is_ge, fill=0.0, base=GC - 1,
                                         pattern=[[GC, P // GC], [0, GC]], channel_multiplier=-1))
            nc.gpsimd.memset(minus_half[:], -0.5).then_inc(const_set, 1)
            pool.wait_ge(ve_set, 1)
            nc.gpsimd.tensor_tensor(rstd[:], ve[:], minus_half[:], ALU.pow).then_inc(rstd_set, 1)
            nc.gpsimd.memset(m_cols[:].rearrange("p a t n -> p (a t n)").bitcast(F32), 0.0).then_inc(mz_set, 1)
            nc.gpsimd.memset(v_sb[:].rearrange("p b t h e -> p (b t h) e")[:, :, D:Q], 1.0).then_inc(ones_set, 1)
            for b in range(1, B):
                nc.gpsimd.memset(k_head[:, b].rearrange("p h b n -> p (h b n)").bitcast(F32), 0.0).then_inc(zeros_set, 1)

        @block.tensor
        def _(pe):
            def scores(b, h):
                u = b * NH + h
                if b == 0:
                    pe.wait_ge(khead_set, u + 1)
                elif h == 0:
                    pe.wait_ge(kd_set[b - 1], 16 * NH)
                pe.wait_ge(qhi_set, b + 1)
                if u >= RS:
                    pe.wait_ge(max_done, u - RS + 1)
                for qt in range(NT):
                    r = (u % RS) * 512 + qt * N
                    mm = nc.tensor.matmul(ps_s[:, r:r + N], q_hi[:, b, qt * P:qt * P + P], k_head[:, b, h, 0, :],
                                          start=True, stop=True)
                mm.then_inc(s_done, 1)

            def scores_t(b, h):
                u = b * NH + h
                if h == 0:
                    pe.wait_ge(qlom_set, b + 1)
                if u < RT:
                    pe.wait_ge(bc_set, 1)
                if u >= RT:
                    pe.wait_ge(exp_done, u - RT + 1)
                for kt in range(NT):
                    r = (u % RT) * 512 + kt * N
                    ks = slice(kt * P, kt * P + P)
                    nc.tensor.matmul(ps_t[:, r:r + N], k_head[:, b, h, 0, ks], q_hi[:, b, :],
                                     start=True, stop=False)
                    mm = nc.tensor.matmul(ps_t[:, r:r + N], k_head[:, b, h, 1, ks], q_lom[:, b, :],
                                          start=False, stop=True)
                mm.then_inc(t_done, 1)

            def q_proj(b):
                pe.wait_ge(h16_set, b + 1)
                if b >= 2:
                    pe.wait_ge(qlom_set, b - 1)
                for part in range(2):
                    mm = nc.tensor.matmul(ps_q[b % 2][:, 0:N], w16[:, part, 0:P], h16[:, b, :],
                                          start=(part == 0), stop=(part == 1))
                mm.then_inc(q_done, 1)

            def k_proj(b):
                pe.wait_ge(h16_set, b + 1)
                if b >= 1:
                    pe.wait_ge(k1_set, b)
                for part in range(2):
                    mm = nc.tensor.matmul(ps_k[:, 0:N], w16[:, part, P:2 * P], h16[:, b, :],
                                          start=(part == 0), stop=(part == 1))
                mm.then_inc(k_done, 1)

            def v_proj(b):
                pe.wait_ge(h16_set, b + 1)
                for kt in range(NT):
                    for part in range(2):
                        r = (b * NT + kt) * C
                        mm = nc.tensor.matmul(ps_o[:, r:r + C], h16[:, b, kt * P:kt * P + P], w16[:, part, 2 * P:2 * P + C],
                                              start=(part == 0), stop=(part == 1))
                if b == B - 1:
                    mm.then_inc(v_done, 1)

            def low_and_max(b):
                ps = ps_q[b % 2]
                nc.tensor.matmul(ps[:, 0:N], minus16[:], q_hi[:, b, :], start=False, stop=True, skip_group_check=True)
                pe.wait_ge(mcols_set, b + 1)
                for qt in range(NT):
                    mm = nc.tensor.matmul(ps[:, qt * P:qt * P + P], m_cols[:, b % 2, qt, :], ident16[:],
                                          start=False, stop=True, skip_group_check=True)
                mm.then_inc(m_done, 1)

            def weighted_values(b):
                if b == 0:
                    pe.wait_ge(v_set, 1)
                    pe.wait_ge(ones_set, 1)
                if b >= 1:
                    pe.wait_ge(fin_set, b)
                pe.wait_ge(exp_done, (b + 1) * NH)
                for kt in range(NT):
                    for h in range(NH):
                        mm = nc.tensor.matmul(ps_o[quad(h), 0:N], v_sb[:, b, kt, h, :],
                                              probs[:, (b * NH + h) % RP, kt * N:kt * N + N],
                                              start=(kt == 0), stop=(kt == NT - 1), skip_group_check=True)
                mm.then_inc(pv_done, 1)

            def turn_out(b):
                pe.wait_ge(o_set, b + 1)
                for qt in range(NT):
                    mm = nc.tensor.transpose(ps_o[:, qt * P:qt * P + P], o_sb[:, b, qt * P:qt * P + P], ident[:])
                mm.then_inc(ot_done, 1)

            def turn_back(b):
                pe.wait_ge(on_set, b + 1)
                for qt in range(NT):
                    mm = nc.tensor.transpose(ps_o[0:C, N + qt * P:N + qt * P + P],
                                             o_n[:, b, qt * NH:qt * NH + NH, :].rearrange("p h d -> p (h d)"), ident[:])
                mm.then_inc(ont_done, 1)

            def project(b):
                pe.wait_ge(ont_set, b + 1)
                nc.tensor.matmul(ps_o[half(b), 0:N], wp_t[:], ont_sb[:, b, :], start=True, stop=True).then_inc(y_done, 1)

            pe.wait_ge(ident_set, 1)
            pe.wait_ge(wqkv_in, 16)
            for p in range(2):
                for t in range(2):
                    mm = nc.tensor.matmul(ps_t[half(p), t * WR:t * WR + WR], w_rows[:, t, :], ident[0:WR, 0:WR],
                                          start=True, stop=True)
            mm.then_inc(wt_done, 1)
            pe.wait_ge(const_set, 1)
            pe.wait_ge(st_set, 1)
            nc.tensor.matmul(ps_o[:, 0:3 * T], group_avg[:], st[:].rearrange("p a t -> p (a t)"),
                             start=True, stop=True).then_inc(gst_done, 1)
            pe.wait_ge(gn_in, 32)
            nc.tensor.transpose(ps_k[:, 0:2], gn_rows[:].rearrange("p a c -> p (a c)"), ident[0:2, 0:2]
                                ).then_inc(gnt_done, 1)
            pe.wait_ge(bh_in, 32)
            nc.tensor.transpose(ps_s[:, 0:2], bh_rows[:].rearrange("p h r d -> p (h r d)"), ident[0:2, 0:2]
                                ).then_inc(bt_done, 1)
            pe.wait_ge(w16_set, 1)
            pe.wait_ge(gnc_set, 1)
            q_proj(0)
            k_proj(0)
            pe.wait_ge(wproj_in, 16)
            pe.wait_ge(bc_in, 32)
            nc.tensor.transpose(ps_t[0:C, 512:512 + C], wp_rows[:], ident[0:C, 0:C])
            nc.tensor.transpose(ps_t[:, 512 + C:512 + C + 2], bc_rows[:].rearrange("p a c -> p (a c)"),
                                ident[0:2, 0:2]).then_inc(wpt_done, 1)
            k_proj(1)
            for s in range(B + 2):
                for h in range(NH):
                    if s < B:
                        scores(s, h)
                    if 1 <= s <= B:
                        scores_t(s - 1, h)
                    if h == 0 and s + 1 < B:
                        q_proj(s + 1)
                    if h == 1 and s + 2 < B:
                        k_proj(s + 2)
                    if s >= 2 and h < 3:
                        (turn_out, turn_back, project)[h](s - 2)
                if s == 0:
                    for b in range(B):
                        v_proj(b)
                if s < B:
                    low_and_max(s)
                if 1 <= s <= B:
                    weighted_values(s - 1)

        @block.vector
        def _(dve):
            n = [0]

            def link(ins):
                n[0] += 1
                ins.then_inc(dve_chain, 1)
                dve.wait_ge(dve_chain, n[0])

            def h_low(b):
                dve.wait_ge(hn_set, b // 2 + 1)
                dve.wait_ge(hhi_set, b + 1)
                nc.vector.tensor_tensor(h16[half(b + 1), b, :], hn[half(b), b // 2, :], h16[half(b), b, :],
                                        ALU.subtract).then_inc(h16_set, 1)

            def k_low(b):
                dve.wait_ge(k2_set, b + 1)
                nc.vector.scalar_tensor_tensor(out=k_all[:, b, 0, :], in0=ps_k[:, 0:N], scalar=b_h[:, 1:2],
                                               in1=k_hi2[:, b % 2, :], op0=ALU.add, op1=ALU.subtract).then_inc(k1_set, 1)

            def row_max(b, h):
                u = b * NH + h
                dve.wait_ge(s_done, u + 1)
                r = (u % RS) * 512
                nc.vector.tensor_reduce(mx[:, b, :, h], ps_s[:, r:r + NT * N].rearrange("p (t n) -> p t n", n=N),
                                        AX_X, ALU.max).then_inc(max_done, 1)

            def max_cols(b):
                dve.wait_ge(max_done, (b + 1) * NH)
                if b == 0:
                    dve.wait_ge(mz_set, 1)
                if b >= 2:
                    dve.wait_ge(m_done, b - 1)
                cols = m_cols[:, b % 2, :, :].rearrange("p t (h e) -> p t h e", e=Q)[:, :, :, D]
                nc.vector.tensor_scalar(cols, mx[:, b, :, :], 1.0 / MS, None, ALU.mult).then_inc(mcols_set, 1)

            def normalise(b):
                dve.wait_ge(ot_done, b + 1)
                ot = ps_o[:, 0:N].rearrange("p (g e) -> p g e", e=Q)
                link(nc.vector.reciprocal(rden[:, b, :], ot[:, :, D]))
                nc.vector.tensor_tensor(o_n[:, b, :, :], ot[:, :, 0:D],
                                        rden[:, b, :].unsqueeze(2).to_broadcast([P, NT * NH, D]),
                                        ALU.mult).then_inc(on_set, 1)

            def residual(b):
                dve.wait_ge(y_done, b + 1)
                nc.vector.scalar_tensor_tensor(out=y_sb[half(b), b // 2, :], in0=ps_o[half(b), 0:N],
                                               scalar=b_c[half(b), 1:2], in1=x_sb[half(b), b // 2, :],
                                               op0=ALU.add, op1=ALU.add).then_inc(fin_set, 1)

            nc.vector.memset(k_head[:, 0].rearrange("p h b n -> p (h b n)").bitcast(F32), 0.0)
            for t in range(T):
                dve.wait_ge(x_in[t], 16)
                link(nc.vector.bn_stats(bn[:, t, :], x_sb[:, t, :]))
            nc.vector.bn_aggr(st[:, 0:2, 0], bn[:, 0, :])
            link(nc.vector.bn_aggr(st[:, 0:2, 1], bn[:, 1, :]))
            nc.vector.tensor_tensor(st[:, 2, :], st[:, 0, :], st[:, 0, :], ALU.mult).then_inc(st_set, 1)
            dve.wait_ge(gst_done, 1)
            link(nc.vector.tensor_copy(gst[:].rearrange("p a t -> p (a t)"), ps_o[:, 0:3 * T]))
            nc.vector.tensor_tensor(ex[:], gst[:, 1, :], gst[:, 2, :], ALU.add)
            link(nc.vector.tensor_tensor(msq[:], gst[:, 0, :], gst[:, 0, :], ALU.mult))
            nc.vector.scalar_tensor_tensor(out=ve[:], in0=ex[:], scalar=EPS, in1=msq[:],
                                           op0=ALU.add, op1=ALU.subtract).then_inc(ve_set, 1)
            dve.wait_ge(gnt_done, 1)
            nc.vector.tensor_copy(gn_c[:], ps_k[:, 0:2]).then_inc(gnc_set, 1)
            nc.vector.tensor_copy(ident16[:], ident[:])
            nc.vector.tensor_scalar(minus16[:], ident[:], -1.0, None, ALU.mult).then_inc(const16_set, 1)
            dve.wait_ge(rstd_set, 1)
            dve.wait_ge(gnc_set, 1)
            link(nc.vector.tensor_scalar(ga[:], rstd[:], gn_c[:, 0:1], None, ALU.mult))
            link(nc.vector.tensor_tensor(mga[:], gst[:, 0, :], ga[:], ALU.mult))
            nc.vector.tensor_scalar(gb[:], mga[:], gn_c[:, 1:2], -1.0, ALU.subtract, ALU.mult).then_inc(gb_set, 1)
            dve.wait_ge(gb_set, 1)
            for t in range(T):
                nc.vector.tensor_scalar(hn[:, t, :], x_sb[:, t, :], ga[:, t:t + 1], gb[:, t:t + 1],
                                        ALU.mult, ALU.add).then_inc(hn_set, 1)
            h_low(0)
            h_low(1)
            dve.wait_ge(whi_set, 1)
            nc.vector.tensor_tensor(w_part(1, 0), wt_qk, w_part(0, 0), ALU.subtract)
            nc.vector.tensor_tensor(w_part(1, 1), wt_v, w_part(0, 1), ALU.subtract).then_inc(w16_set, 1)
            iq = ident[:].rearrange("p (h r d) -> p h r d", r=2, d=D)
            nc.vector.tensor_reduce(half_cols[:, 0:1], iq[:, :, 0, :], mybir.AxisListType.XY, ALU.add)
            nc.vector.tensor_reduce(half_cols[:, 1:2], iq[:, :, 1, :], mybir.AxisListType.XY, ALU.add)
            nc.vector.tensor_reduce(half_cols[:, 2:3], iq[:, :, 1, 0], AX_X, ALU.add)
            dve.wait_ge(bt_done, 1)
            link(nc.vector.tensor_copy(b_h[:], ps_s[:, 0:2]))
            nc.vector.tensor_tensor(kb[:, 0:1], b_h[:, 1:2], half_cols[:, 1:2], ALU.mult)
            link(nc.vector.tensor_tensor(kb[:, 1:2], b_h[:, 1:2], half_cols[:, 0:1], ALU.mult))
            nc.vector.scalar_tensor_tensor(out=kb[:, 1:2], in0=half_cols[:, 2:3], scalar=-MS, in1=kb[:, 1:2],
                                           op0=ALU.mult, op1=ALU.add).then_inc(bh_set, 1)
            k_low(0)
            dve.wait_ge(k1_set, 1)
            for h in range(NH):
                nc.vector.tensor_copy(k_head[quad(h), 0, h, :, :], k_all[quad(h), 0, :, :]).then_inc(khead_set, 1)
            h_low(2)
            h_low(3)
            k_low(1)
            dve.wait_ge(wpt_done, 1)
            nc.vector.tensor_copy(wp_t[:], ps_t[0:C, 512:512 + C])
            nc.vector.tensor_copy(b_c[:], ps_t[:, 512 + C:512 + C + 2]).then_inc(bc_set, 1)
            for s in range(B + 2):
                for h in range(NH):
                    if s < B:
                        row_max(s, h)
                    if h == 1 and s + 2 < B:
                        k_low(s + 2)
                    if s >= 2 and h in (0, 2):
                        (normalise, None, residual)[h](s - 2)
                if s < B:
                    max_cols(s)
                if s == 0:
                    dve.wait_ge(v_done, 1)
                    nc.vector.tensor_copy(v_sb[:].rearrange("p b t h e -> p (b t h) e")[:, :, 0:D],
                                          ps_o[:, :].rearrange("p (g d) -> p g d", d=D)).then_inc(v_set, 1)

        @block.scalar
        def _(act):
            def h_high(b):
                act.wait_ge(gb_set, 1)
                t = b // 2
                nc.scalar.activation(h16[half(b), b, :], x_sb[half(b), t, :], ACT.Identity, bias=gb[half(b), t:t + 1],
                                     scale=ga[half(b), t:t + 1]).then_inc(hhi_set, 1)

            def q_high(b):
                act.wait_ge(q_done, b + 1)
                nc.scalar.activation(q_hi[:, b, :], ps_q[b % 2][:, 0:N], ACT.Identity, bias=b_h[:, 0:1]).then_inc(qhi_set, 1)

            def k_high(b):
                act.wait_ge(k_done, b + 1)
                if b >= 2:
                    act.wait_ge(k1_set, b - 1)
                nc.scalar.activation(k_hi2[:, b % 2, :], ps_k[:, 0:N], ACT.Identity, bias=kb[:, 0:1],
                                     scale=half_cols[:, 1:2])
                nc.scalar.activation(k_all[:, b, 1, :], ps_k[:, 0:N], ACT.Identity, bias=kb[:, 1:2],
                                     scale=half_cols[:, 0:1]).then_inc(k2_set, 1)

            def soft_exp(b, h):
                u = b * NH + h
                act.wait_ge(t_done, u + 1)
                if u >= RP:
                    act.wait_ge(pv_done, (u - RP) // NH + 1)
                r = (u % RT) * 512
                nc.scalar.activation(probs[:, u % RP, :], ps_t[:, r:r + NT * N], ACT.Exp, scale=SCALE
                                     ).then_inc(exp_done, 1)

            def q_low_max(b):
                act.wait_ge(m_done, b + 1)
                nc.scalar.activation(q_lom[:, b, :], ps_q[b % 2][:, 0:N], ACT.Identity, bias=b_h[:, 0:1]
                                     ).then_inc(qlom_set, 1)

            def save_out(b):
                act.wait_ge(pv_done, b + 1)
                nc.scalar.activation(o_sb[:, b, :], ps_o[:, 0:N], ACT.Copy).then_inc(o_set, 1)

            def save_turned(b):
                act.wait_ge(ont_done, b + 1)
                nc.scalar.activation(ont_sb[:, b, :], ps_o[0:C, N:2 * N], ACT.Identity, bias=b_c[0:C, 0:1]
                                     ).then_inc(ont_set, 1)

            act.wait_ge(wt_done, 1)
            nc.scalar.activation(w_part(0, 0), wt_qk, ACT.Copy)
            nc.scalar.activation(w_part(0, 1), wt_v, ACT.Copy).then_inc(whi_set, 1)
            for b in range(B):
                h_high(b)
            act.wait_ge(bh_set, 1)
            q_high(0)
            k_high(0)
            k_high(1)
            for s in range(B + 2):
                for h in range(NH):
                    if 1 <= s <= B:
                        soft_exp(s - 1, h)
                    if h == 0 and s + 1 < B:
                        q_high(s + 1)
                    if h == 1 and s + 2 < B:
                        k_high(s + 2)
                    if h == 1 and s >= 2:
                        save_turned(s - 2)
                if s < B:
                    q_low_max(s)
                if 1 <= s <= B:
                    save_out(s - 1)


_INS = ['x', 'L0_conv_gn_w', 'L0_conv_gn_b', 'L0_conv_w_qkv', 'L0_conv_b_qkv', 'L0_conv_w_proj', 'L0_conv_b_proj']
_OUTS = [((4, 64, 16, 16), 'float32')]


def kernel(**inputs):
    import numpy as _np
    import concourse.bacc as _bacc
    from concourse import mybir as _mybir
    from concourse.bass_utils import run_bass_kernel_spmd as _run

    nc = _bacc.Bacc("TRN2", target_bir_lowering=False, num_devices=1)
    arrays, args = {}, []
    for name in _INS:
        a = _np.ascontiguousarray(inputs[name])
        arrays[f"in_{name}_dram"] = a
        args.append(nc.dram_tensor(f"in_{name}_dram", a.shape, _mybir.dt.from_np(a.dtype), kind="ExternalInput").ap())
    for i, (shape, dtype) in enumerate(_OUTS):
        dt = _mybir.dt.from_np(_np.dtype(dtype))
        args.append(nc.dram_tensor(f"out_{i}_dram", shape, dt, kind="ExternalOutput").ap())
    groupnorm_attention(nc, *args)
    r = _run(nc, [arrays], core_ids=[0])
    got = tuple(r.results[0][f"out_{i}_dram"] for i in range(len(_OUTS)))
    return got[0]
```

```python
from contextlib import ExitStack

import concourse.bass as bass
from concourse import mybir

ALU = mybir.AluOpType
ACT = mybir.ActivationFunctionType
AX_X = mybir.AxisListType.X
F32 = mybir.dt.float32
F16 = mybir.dt.float16


def groupnorm_attention(
    nc: bass.Bass,
    x: bass.AP,
    gn_w: bass.AP,
    gn_b: bass.AP,
    w_qkv: bass.AP,
    b_qkv: bass.AP,
    w_proj: bass.AP,
    b_proj: bass.AP,
    out: bass.AP,
):
    P = 128
    B, C, HH, WW = x.shape
    N = HH * WW
    NH = 4
    D = C // NH
    GROUPS = 8
    GC = C // GROUPS
    EPS = 1e-5
    SCALE = 1.0 / float(D) ** 0.5
    T = B // 2
    NT = N // P
    Q = P // NH
    MS = 64.0
    RS = 2
    RT = 2
    RP = 8
    assert C * 2 == P and D * 2 == Q and N == 2 * P and B == 4

    x_v = x.rearrange("(t p) c h w -> (p c) t (h w)", p=2)
    out_v = out.rearrange("(t p) c h w -> (p c) t (h w)", p=2)
    WR = 3 * C // 2

    with ExitStack() as ctx:
        def sb(name, shape, dt):
            return ctx.enter_context(nc.sbuf_tensor(name, shape, dt))

        def psum(name, cols):
            return ctx.enter_context(nc.psum_tensor(name, [P, cols], F32))

        def sem(name):
            return ctx.enter_context(nc.semaphore(name))

        x_sb = sb("x_sb", [P, T, N], F32)
        w_rows = sb("w_rows", [WR, 2, C], F32)
        wp_rows = sb("wp_rows", [C, C], F32)
        gn_rows = sb("gn_rows", [2, 2, C], F32)
        bh_rows = sb("bh_rows", [2, NH, 2, D], F32)
        bc_rows = sb("bc_rows", [2, 2, C], F32)
        ident = sb("ident", [P, P], F32)
        zeros = sb("zeros", [P, 512], F16)
        ident16 = sb("ident16", [P, P], F16)
        minus16 = sb("minus16", [P, P], F16)
        group_avg = sb("group_avg", [P, P], F32)
        minus_half = sb("minus_half", [P, 1], F32)
        half_cols = sb("half_cols", [P, 3], F32)
        gn_c = sb("gn_c", [P, 2], F32)
        b_h = sb("b_h", [P, 2], F32)
        b_c = sb("b_c", [P, 2], F32)
        b_y = sb("b_y", [P, 1], F32)
        kb = sb("kb", [P, 2], F32)
        w16 = sb("w16", [P, 2, 5 * C], F16)
        wp_t = sb("wp_t", [C, C], F32)
        bn = sb("bn", [P, T, 6], F32)
        st = sb("st", [P, T, 3], F32)
        msq = sb("msq", [P, T], F32)
        ve = sb("ve", [P, T], F32)
        rstd = sb("rstd", [P, T], F32)
        mw = sb("mw", [P, T], F32)
        ga = sb("ga", [P, T], F32)
        gb = sb("gb", [P, T], F32)
        hn = sb("hn", [P, T, N], F32)
        h16 = sb("h16", [P, B, N], F16)
        q_hi = sb("q_hi", [P, B, N], F16)
        q_lom = sb("q_lom", [P, B, N], F16)
        k_hi2 = sb("k_hi2", [P, B, N], F16)
        k_all = sb("k_all", [P, B, 2, N], F16)
        k_head = sb("k_head", [P, B, NH, 2, N], F16)
        v_sb = sb("v_sb", [P, B, NT, NH, Q], F32)
        mx = sb("mx", [P, B, NT, NH], F32)
        m_cols = sb("m_cols", [P, 2, NT, P], F16)
        probs = sb("probs", [P, RP, NT * N], F32)
        o_sb = sb("o_sb", [P, B, N], F32)
        rden = sb("rden", [P, B, NT * NH], F32)
        o_n = sb("o_n", [P, B, NT * NH, D], F32)
        ont_sb = sb("ont_sb", [C, B, N], F32)
        xb = sb("xb", [P, T, N], F32)
        y_sb = sb("y_sb", [P, T, N], F32)

        ps_s = psum("ps_s", RS * 512)
        ps_t = psum("ps_t", RT * 512)
        ps_q = [psum(f"ps_q{i}", 512) for i in range(2)]
        ps_k = psum("ps_k", 512)
        ps_o = psum("ps_o", 512)

        x_in = [sem(f"x_in{t}") for t in range(T)]
        wqkv_in = sem("wqkv_in")
        wproj_in = sem("wproj_in")
        gn_in = sem("gn_in")
        bh_in = sem("bh_in")
        bc_in = sem("bc_in")
        ident_set = sem("ident_set")
        const_set = sem("const_set")
        pool_chain = sem("pool_chain")
        zeros_set = sem("zeros_set")
        mz_set = sem("mz_set")
        ones_set = sem("ones_set")
        bh_set = sem("bh_set")
        bias_set = sem("bias_set")
        bn_set = sem("bn_set")
        half_set = sem("half_set")
        zt_set = sem("zt_set")
        khi_set = sem("khi_set")
        dve_chain = sem("dve_chain")
        wt_done = sem("wt_done")
        gnt_done = sem("gnt_done")
        bt_done = sem("bt_done")
        wpt_done = sem("wpt_done")
        gnc_set = sem("gnc_set")
        bc_set = sem("bc_set")
        by_done = sem("by_done")
        by_set = sem("by_set")
        xb_set = sem("xb_set")
        const16_set = sem("const16_set")
        whi_set = sem("whi_set")
        w16_set = sem("w16_set")
        st_set = sem("st_set")
        gst_done = sem("gst_done")
        ve_set = sem("ve_set")
        rstd_set = sem("rstd_set")
        hn_set = sem("hn_set")
        hn1_set = sem("hn1_set")
        hlow_set = sem("hlow_set")
        mw_set = sem("mw_set")
        gb_set = sem("gb_set")
        hhi_set = sem("hhi_set")
        h16_set = sem("h16_set")
        q_done = sem("q_done")
        k_done = sem("k_done")
        qhi_set = sem("qhi_set")
        k2_set = sem("k2_set")
        k1_set = sem("k1_set")
        v_done = sem("v_done")
        v_set = sem("v_set")
        kd_set = [[sem(f"kd_set{b}_{h}") for h in range(NH)] for b in range(B)]
        s_done = sem("s_done")
        max_done = sem("max_done")
        mcols_set = sem("mcols_set")
        m_done = sem("m_done")
        qlom_set = sem("qlom_set")
        t_done = sem("t_done")
        exp_done = sem("exp_done")
        pv_done = sem("pv_done")
        o_set = sem("o_set")
        ot_done = sem("ot_done")
        on_set = sem("on_set")
        ont_done = sem("ont_done")
        ont_set = sem("ont_set")
        y_done = sem("y_done")
        fin_set = sem("fin_set")
        out_done = sem("out_done")

        def half(b):
            return slice((b % 2) * C, (b % 2) * C + C)

        gst = (ps_o[:, 0:3], ps_q[1][:, 0:3])

        def t_bank(b, h):
            if b == B - 1 and h >= RT:
                return ps_s[:, (h - RT) * 512:(h - RT) * 512 + 512]
            r = (b * NH + h) % RT * 512
            return ps_t[:, r:r + 512]

        def out_bank(b):
            return ps_k if b % 2 else ps_o

        def quad(h):
            return slice(h * Q, h * Q + Q)

        wt_qk = ps_t[:, 0:2 * C].rearrange("p (g d) -> p g d", d=D).unsqueeze(2).to_broadcast([P, 2 * NH, 2, D])
        wt_v = ps_t[:, 2 * C:3 * C]

        def w_part(part, v):
            if v:
                return w16[:, part, 4 * C:5 * C]
            return w16[:, part, 0:4 * C].rearrange("p (g r d) -> p g r d", r=2, d=D)

        block = ctx.enter_context(nc.Block())

        @block.sync
        def _(sp):
            sp.dma_start(x_sb[:, 0, :], x_v[:, 0, :]).then_inc(x_in[0], 16)
            sp.dma_start(w_rows[:], w_qkv.rearrange("(t p) c -> p t c", t=2)).then_inc(wqkv_in, 16)
            sp.dma_start(x_sb[:, 1, :], x_v[:, 1, :]).then_inc(x_in[1], 16)
            for i, src in enumerate((gn_w, gn_b)):
                sp.dma_start(gn_rows[i:i + 1], src.rearrange("(a c) -> a c", a=1).unsqueeze(1).to_broadcast([1, 2, C])
                             ).then_inc(gn_in, 16)
            for i in range(2):
                src = b_qkv[i * C:i * C + C].rearrange("(a h d) -> a h d", a=1, h=NH)
                sp.dma_start(bh_rows[i:i + 1], src.unsqueeze(2).to_broadcast([1, NH, 2, D])).then_inc(bh_in, 16)
            sp.dma_start(wp_rows[:], w_proj).then_inc(wproj_in, 16)
            for i, src in enumerate((b_qkv[2 * C:3 * C], b_proj)):
                sp.dma_start(bc_rows[i:i + 1], src.rearrange("(a c) -> a c", a=1).unsqueeze(1).to_broadcast([1, 2, C])
                             ).then_inc(bc_in, 16)
            for b in range(B):
                sp.wait_ge(k1_set, b + 1)
                sp.wait_ge(k2_set, b + 1)
                sp.wait_ge(zeros_set, b + 1)
                for h in range(NH):
                    sp.dma_start(k_head[quad(h), b, h, :, :], k_all[quad(h), b, :, :]).then_inc(kd_set[b][h], 16)
            for t in range(T):
                sp.wait_ge(fin_set, 2 * t + 2)
                sp.dma_start(out_v[:, t, :], y_sb[:, t, :]).then_inc(out_done, 16)
            sp.wait_ge(out_done, 16 * T)

        @block.gpsimd
        def _(pool):
            n = [0]

            def link(ins):
                n[0] += 1
                ins.then_inc(pool_chain, 1)
                pool.wait_ge(pool_chain, n[0])

            link(nc.gpsimd.memset(ident[:], 0.0))
            nc.gpsimd.affine_select(out=ident[:], in_=ident[:], compare_op=ALU.not_equal, fill=1.0, base=0,
                                    pattern=[[-1, P]], channel_multiplier=1).then_inc(ident_set, 1)
            link(nc.gpsimd.memset(group_avg[:], 1.0 / GC))
            ga_v = group_avg[:].rearrange("p (g c) -> p g c", c=GC)
            link(nc.gpsimd.affine_select(out=ga_v, in_=ga_v, compare_op=ALU.is_ge, fill=0.0, base=0,
                                         pattern=[[-GC, P // GC], [0, GC]], channel_multiplier=1))
            link(nc.gpsimd.affine_select(out=ga_v, in_=ga_v, compare_op=ALU.is_ge, fill=0.0, base=GC - 1,
                                         pattern=[[GC, P // GC], [0, GC]], channel_multiplier=-1))
            nc.gpsimd.memset(minus_half[:], -0.5).then_inc(const_set, 1)

            def zero_keys(b):
                nc.gpsimd.memset(k_head[:, b].rearrange("p h b n -> p (h b n)").bitcast(F32), 0.0).then_inc(zeros_set, 1)

            def reciprocal_root(t):
                pool.wait_ge(ve_set, t + 1)
                nc.gpsimd.tensor_tensor(rstd[:, t:t + 1], ve[:, t:t + 1], minus_half[:], ALU.pow).then_inc(rstd_set, 1)

            zero_keys(0)
            zero_keys(1)
            reciprocal_root(0)
            nc.gpsimd.memset(m_cols[:].rearrange("p a t n -> p (a t n)").bitcast(F32), 0.0).then_inc(mz_set, 1)
            reciprocal_root(1)
            pool.wait_ge(gb_set, 2)
            nc.gpsimd.tensor_scalar(hn[:, 1, :], x_sb[:, 1, :], ga[:, 1:2], gb[:, 1:2], ALU.mult, ALU.add
                                    ).then_inc(hn1_set, 1)
            pool.wait_ge(hn1_set, 1)
            for b in range(2, B):
                pool.wait_ge(hhi_set, b + 1)
                nc.gpsimd.tensor_tensor(h16[half(b + 1), b, :], hn[half(b), 1, :], h16[half(b), b, :],
                                        ALU.subtract).then_inc(hlow_set, 1)
            pool.wait_ge(hlow_set, 2)
            nc.gpsimd.memset(v_sb[:].rearrange("p b t h e -> p (b t h) e")[:, :, D:Q], 1.0).then_inc(ones_set, 1)
            zero_keys(2)
            zero_keys(3)
            pool.wait_ge(by_set, 1)
            for t in range(T):
                nc.gpsimd.tensor_scalar(xb[:, t, :], x_sb[:, t, :], b_y[:], None, ALU.add).then_inc(xb_set, 1)

        @block.tensor
        def _(pe):
            def scores(b, h):
                u = b * NH + h
                pe.wait_ge(khi_set, b + 1)
                pe.wait_ge(qhi_set, b + 1)
                if u >= RS:
                    pe.wait_ge(max_done, u - RS + 1)
                for qt in range(NT):
                    r = (u % RS) * 512 + qt * N
                    mm = nc.tensor.matmul(ps_s[:, r:r + N], q_hi[quad(h), b, qt * P:qt * P + P], k_hi2[quad(h), b, :],
                                          start=True, stop=True)
                mm.then_inc(s_done, 1)

            def scores_t(b, h):
                u = b * NH + h
                pe.wait_ge(kd_set[b][h], 16)
                if h == 0:
                    pe.wait_ge(qlom_set, b + 1)
                if u < RT:
                    pe.wait_ge(by_set, 1)
                if b == B - 1 and h >= RT:
                    pe.wait_ge(max_done, u + 1)
                elif u >= RT:
                    pe.wait_ge(exp_done, u - RT + 1)
                for kt in range(NT):
                    bank, r = t_bank(b, h), kt * N
                    ks = slice(kt * P, kt * P + P)
                    nc.tensor.matmul(bank[:, r:r + N], k_head[:, b, h, 0, ks], q_hi[:, b, :],
                                     start=True, stop=False)
                    mm = nc.tensor.matmul(bank[:, r:r + N], k_head[:, b, h, 1, ks], q_lom[:, b, :],
                                          start=False, stop=True)
                mm.then_inc(t_done, 1)

            def wait_input(b):
                if b < 2:
                    pe.wait_ge(h16_set, b + 1)
                else:
                    pe.wait_ge(hlow_set, b - 1)

            def q_proj(b):
                wait_input(b)
                if b >= 2:
                    pe.wait_ge(qlom_set, b - 1)
                for part in range(2):
                    mm = nc.tensor.matmul(ps_q[b % 2][:, 0:N], w16[:, part, 0:P], h16[:, b, :],
                                          start=(part == 0), stop=(part == 1))
                mm.then_inc(q_done, 1)

            def k_proj(b):
                wait_input(b)
                if b >= 1:
                    pe.wait_ge(k1_set, b)
                    pe.wait_ge(k2_set, b)
                for part in range(2):
                    mm = nc.tensor.matmul(ps_k[:, 0:N], w16[:, part, P:2 * P], h16[:, b, :],
                                          start=(part == 0), stop=(part == 1))
                mm.then_inc(k_done, 1)

            def v_proj(b):
                wait_input(b)
                pe.wait_ge(w16_set, 2)
                for kt in range(NT):
                    for part in range(2):
                        r = (b * NT + kt) * C
                        mm = nc.tensor.matmul(ps_o[:, r:r + C], h16[:, b, kt * P:kt * P + P], w16[:, part, 2 * P:2 * P + C],
                                              start=(part == 0), stop=(part == 1))
                if b == B - 1:
                    mm.then_inc(v_done, 1)

            def low_and_max(b):
                ps = ps_q[b % 2]
                if b == 0:
                    pe.wait_ge(const16_set, 1)
                nc.tensor.matmul(ps[:, 0:N], minus16[:], q_hi[:, b, :], start=False, stop=True, skip_group_check=True)
                pe.wait_ge(mcols_set, b + 1)
                for qt in range(NT):
                    mm = nc.tensor.matmul(ps[:, qt * P:qt * P + P], m_cols[:, b % 2, qt, :], ident16[:],
                                          start=False, stop=True, skip_group_check=True)
                mm.then_inc(m_done, 1)

            def weighted_values(b, kt):
                if kt == 0:
                    if b == 0:
                        pe.wait_ge(v_set, 1)
                        pe.wait_ge(ones_set, 1)
                    if b == 1:
                        pe.wait_ge(k2_set, B)
                    if b >= 2:
                        pe.wait_ge(fin_set, b - 1)
                    pe.wait_ge(exp_done, (b + 1) * NH)
                for h in range(NH):
                    mm = nc.tensor.matmul(out_bank(b)[quad(h), 0:N], v_sb[:, b, kt, h, :],
                                          probs[:, (b * NH + h) % RP, kt * N:kt * N + N],
                                          start=(kt == 0), stop=(kt == NT - 1), skip_group_check=True)
                if kt == NT - 1:
                    mm.then_inc(pv_done, 1)

            def turn_out(b):
                pe.wait_ge(o_set, b + 1)
                for qt in range(NT):
                    mm = nc.tensor.transpose(out_bank(b)[:, qt * P:qt * P + P], o_sb[:, b, qt * P:qt * P + P], ident[:])
                mm.then_inc(ot_done, 1)

            def turn_back(b):
                pe.wait_ge(on_set, b + 1)
                for qt in range(NT):
                    mm = nc.tensor.transpose(out_bank(b)[0:C, N + qt * P:N + qt * P + P],
                                             o_n[:, b, qt * NH:qt * NH + NH, :].rearrange("p h d -> p (h d)"), ident[:])
                mm.then_inc(ont_done, 1)

            def project(b):
                pe.wait_ge(ont_set, b + 1)
                nc.tensor.matmul(out_bank(b)[half(b), 0:N], wp_t[:], ont_sb[:, b, :], start=True, stop=True).then_inc(y_done, 1)

            def keep_busy(bank, products):
                for _ in range(products):
                    nc.tensor.matmul(bank, zeros[:, 0:P], zeros[:], start=True, stop=True)

            def turn_parameters():
                pe.wait_ge(w16_set, 2)
                pe.wait_ge(wproj_in, 16)
                pe.wait_ge(bc_in, 32)
                nc.tensor.transpose(ps_t[0:C, 512:512 + C], wp_rows[:], ident[0:C, 0:C])
                nc.tensor.transpose(ps_t[:, 512 + C:512 + C + 2], bc_rows[:].rearrange("p a c -> p (a c)"),
                                    ident[0:2, 0:2]).then_inc(wpt_done, 1)

            def project_bias():
                pe.wait_ge(bc_set, 1)
                for p in range(2):
                    mm = nc.tensor.matmul(ps_t[half(p), 512:513], wp_t[:], b_c[0:C, 0:1], start=True, stop=True)
                mm.then_inc(by_done, 1)

            def group_statistics(t):
                pe.wait_ge(st_set, t + 1)
                nc.tensor.matmul(gst[t], group_avg[:], st[:, t, :], start=True, stop=True).then_inc(gst_done, 1)

            pe.wait_ge(const_set, 1)
            group_statistics(0)
            pe.wait_ge(ident_set, 1)
            pe.wait_ge(wqkv_in, 16)
            for p in range(2):
                for t in range(2):
                    mm = nc.tensor.matmul(ps_t[half(p), t * WR:t * WR + WR], w_rows[:, t, :], ident[0:WR, 0:WR],
                                          start=True, stop=True)
            mm.then_inc(wt_done, 1)
            pe.wait_ge(gn_in, 32)
            nc.tensor.transpose(ps_k[:, 0:2], gn_rows[:].rearrange("p a c -> p (a c)"), ident[0:2, 0:2]
                                ).then_inc(gnt_done, 1)
            group_statistics(1)
            pe.wait_ge(zt_set, 1)
            keep_busy(ps_s[:, 512:1024], 1)
            pe.wait_ge(bh_in, 32)
            nc.tensor.transpose(ps_s[:, 0:2], bh_rows[:].rearrange("p h r d -> p (h r d)"), ident[0:2, 0:2]
                                ).then_inc(bt_done, 1)
            keep_busy(ps_s[:, 512:1024], 3)
            pe.wait_ge(w16_set, 1)
            pe.wait_ge(gnc_set, 1)
            k_proj(0)
            q_proj(0)
            turn_parameters()
            v_proj(0)
            q_proj(1)
            scores(0, 0)
            scores(0, 1)
            k_proj(1)
            scores(0, 2)
            project_bias()
            scores(0, 3)
            keep_busy(ps_t[:, 0:512], 2)
            v_proj(1)
            k_proj(2)
            v_proj(2)
            v_proj(3)
            low_and_max(0)
            keep_busy(ps_t[:, 0:512], 1)
            scores(1, 0)
            scores(1, 1)
            q_proj(2)
            scores_t(0, 0)
            scores(1, 2)
            scores_t(0, 1)
            k_proj(3)
            scores(1, 3)
            scores_t(0, 2)
            scores_t(0, 3)
            low_and_max(1)
            scores(2, 0)
            scores(2, 1)
            for kt in range(NT):
                weighted_values(0, kt)
            scores(2, 2)
            scores_t(1, 0)
            scores(2, 3)
            turn_out(0)
            scores_t(1, 1)
            scores_t(1, 2)
            turn_back(0)
            q_proj(3)
            scores_t(1, 3)
            low_and_max(2)
            project(0)
            scores(3, 0)
            scores(3, 1)
            scores_t(2, 0)
            for kt in range(NT):
                weighted_values(1, kt)
            scores(3, 2)
            scores_t(2, 1)
            turn_out(1)
            scores(3, 3)
            scores_t(2, 2)
            turn_back(1)
            scores_t(2, 3)
            low_and_max(3)
            project(1)
            scores_t(3, 0)
            scores_t(3, 1)
            scores_t(3, 2)
            scores_t(3, 3)
            for kt in range(NT):
                weighted_values(2, kt)
            weighted_values(3, 0)
            turn_out(2)
            weighted_values(3, 1)
            turn_back(2)
            turn_out(3)
            project(2)
            turn_back(3)
            project(3)

        @block.vector
        def _(dve):
            n = [0]

            def link(ins):
                n[0] += 1
                ins.then_inc(dve_chain, 1)
                dve.wait_ge(dve_chain, n[0])

            def h_low(b):
                dve.wait_ge(hn_set, 1)
                dve.wait_ge(hhi_set, b + 1)
                nc.vector.tensor_tensor(h16[half(b + 1), b, :], hn[half(b), b // 2, :], h16[half(b), b, :],
                                        ALU.subtract).then_inc(h16_set, 1)

            def k_low(b):
                dve.wait_ge(khi_set, b + 1)
                nc.vector.scalar_tensor_tensor(out=k_all[:, b, 0, :], in0=ps_k[:, 0:N], scalar=b_h[:, 1:2],
                                               in1=k_hi2[:, b, :], op0=ALU.add, op1=ALU.subtract).then_inc(k1_set, 1)

            def row_max(b, h):
                u = b * NH + h
                dve.wait_ge(s_done, u + 1)
                r = (u % RS) * 512
                nc.vector.tensor_reduce(mx[:, b, :, h], ps_s[:, r:r + NT * N].rearrange("p (t n) -> p t n", n=N),
                                        AX_X, ALU.max).then_inc(max_done, 1)

            def max_cols(b):
                dve.wait_ge(max_done, (b + 1) * NH)
                if b == 0:
                    dve.wait_ge(mz_set, 1)
                if b >= 2:
                    dve.wait_ge(m_done, b - 1)
                cols = m_cols[:, b % 2, :, :].rearrange("p t (h e) -> p t h e", e=Q)[:, :, :, D]
                nc.vector.tensor_scalar(cols, mx[:, b, :, :], 1.0 / MS, None, ALU.mult).then_inc(mcols_set, 1)

            def normalise(b):
                dve.wait_ge(ot_done, b + 1)
                ot = out_bank(b)[:, 0:N].rearrange("p (g e) -> p g e", e=Q)
                link(nc.vector.reciprocal(rden[:, b, :], ot[:, :, D]))
                nc.vector.tensor_tensor(o_n[:, b, :, :], ot[:, :, 0:D],
                                        rden[:, b, :].unsqueeze(2).to_broadcast([P, NT * NH, D]),
                                        ALU.mult).then_inc(on_set, 1)

            def residual(b):
                dve.wait_ge(y_done, b + 1)
                dve.wait_ge(xb_set, b // 2 + 1)
                nc.vector.tensor_tensor(y_sb[half(b), b // 2, :], out_bank(b)[half(b), 0:N], xb[half(b), b // 2, :],
                                        ALU.add).then_inc(fin_set, 1)

            def save_parameters():
                dve.wait_ge(wpt_done, 1)
                nc.vector.tensor_copy(wp_t[:], ps_t[0:C, 512:512 + C])
                nc.vector.tensor_copy(b_c[:], ps_t[:, 512 + C:512 + C + 2]).then_inc(bc_set, 1)

            def output_bias():
                dve.wait_ge(by_done, 1)
                nc.vector.tensor_tensor(b_y[:], ps_t[:, 512:513], b_c[:, 1:2], ALU.add).then_inc(by_set, 1)

            def save_values():
                dve.wait_ge(v_done, 1)
                nc.vector.tensor_copy(v_sb[:].rearrange("p b t h e -> p (b t h) e")[:, :, 0:D],
                                      ps_o[:, :].rearrange("p (g d) -> p g d", d=D)).then_inc(v_set, 1)

            nc.vector.memset(zeros[:].bitcast(F32), 0.0).then_inc(zt_set, 1)
            dve.wait_ge(ident_set, 1)
            nc.vector.tensor_copy(ident16[:], ident[:])
            nc.vector.tensor_scalar(minus16[:], ident[:], -1.0, None, ALU.mult).then_inc(const16_set, 1)
            iq = ident[:].rearrange("p (h r d) -> p h r d", r=2, d=D)
            nc.vector.tensor_reduce(half_cols[:, 0:1], iq[:, :, 0, :], mybir.AxisListType.XY, ALU.add)
            nc.vector.tensor_reduce(half_cols[:, 1:2], iq[:, :, 1, :], mybir.AxisListType.XY, ALU.add)
            nc.vector.tensor_reduce(half_cols[:, 2:3], iq[:, :, 1, 0], AX_X, ALU.add).then_inc(half_set, 1)

            def channel_statistics(t):
                dve.wait_ge(bn_set, t + 1)
                link(nc.vector.bn_aggr(st[:, t, 0:2], bn[:, t, :]))
                nc.vector.scalar_tensor_tensor(out=st[:, t, 2:3], in0=st[:, t, 0:1], scalar=st[:, t, 0:1],
                                               in1=st[:, t, 1:2], op0=ALU.mult, op1=ALU.add).then_inc(st_set, 1)

            def group_variance(t):
                dve.wait_ge(gst_done, t + 1)
                link(nc.vector.tensor_scalar(msq[:, t:t + 1], gst[t][:, 0:1], gst[t][:, 0:1], None, ALU.mult))
                nc.vector.scalar_tensor_tensor(out=ve[:, t:t + 1], in0=gst[t][:, 2:3], scalar=EPS, in1=msq[:, t:t + 1],
                                               op0=ALU.add, op1=ALU.subtract).then_inc(ve_set, 1)

            def mean_weight(t):
                nc.vector.scalar_tensor_tensor(out=mw[:, t:t + 1], in0=gst[t][:, 0:1], scalar=-1.0, in1=gn_c[:, 0:1],
                                               op0=ALU.mult, op1=ALU.mult).then_inc(mw_set, 1)

            def scale_and_shift(t):
                dve.wait_ge(rstd_set, t + 1)
                dve.wait_ge(mw_set, t + 1)
                nc.vector.tensor_tensor(ga[:, t:t + 1], rstd[:, t:t + 1], gn_c[:, 0:1], ALU.mult)
                nc.vector.tensor_scalar(gb[:, t:t + 1], mw[:, t:t + 1], rstd[:, t:t + 1], gn_c[:, 1:2],
                                        ALU.mult, ALU.add).then_inc(gb_set, 1)

            def channel_sums(t):
                dve.wait_ge(x_in[t], 16)
                nc.vector.bn_stats(bn[:, t, :], x_sb[:, t, :]).then_inc(bn_set, 1)

            channel_sums(0)
            channel_statistics(0)
            channel_sums(1)
            group_variance(0)
            channel_statistics(1)
            dve.wait_ge(gnt_done, 1)
            nc.vector.tensor_copy(gn_c[:], ps_k[:, 0:2]).then_inc(gnc_set, 1)
            dve.wait_ge(gnc_set, 1)
            mean_weight(0)
            scale_and_shift(0)
            dve.wait_ge(gb_set, 1)
            nc.vector.tensor_scalar(hn[:, 0, :], x_sb[:, 0, :], ga[:, 0:1], gb[:, 0:1], ALU.mult, ALU.add
                                    ).then_inc(hn_set, 1)
            dve.wait_ge(whi_set, 1)
            nc.vector.tensor_tensor(w_part(1, 0), wt_qk, w_part(0, 0), ALU.subtract).then_inc(w16_set, 1)
            h_low(0)
            nc.vector.tensor_tensor(w_part(1, 1), wt_v, w_part(0, 1), ALU.subtract).then_inc(w16_set, 1)
            dve.wait_ge(bt_done, 1)
            dve.wait_ge(half_set, 1)
            nc.vector.tensor_copy(b_h[:], ps_s[:, 0:2]).then_inc(bias_set, 1)
            group_variance(1)
            dve.wait_ge(bias_set, 1)
            nc.vector.tensor_tensor(kb[:, 0:1], b_h[:, 1:2], half_cols[:, 1:2], ALU.mult).then_inc(bh_set, 1)
            nc.vector.tensor_tensor(kb[:, 1:2], b_h[:, 1:2], half_cols[:, 0:1], ALU.mult).then_inc(bias_set, 1)
            mean_weight(1)
            h_low(1)
            dve.wait_ge(bias_set, 2)
            nc.vector.scalar_tensor_tensor(out=kb[:, 1:2], in0=half_cols[:, 2:3], scalar=-MS, in1=kb[:, 1:2],
                                           op0=ALU.mult, op1=ALU.add).then_inc(bh_set, 1)
            scale_and_shift(1)
            k_low(0)
            save_parameters()
            row_max(0, 0)
            row_max(0, 1)
            k_low(1)
            row_max(0, 2)
            row_max(0, 3)
            max_cols(0)
            output_bias()
            k_low(2)
            row_max(1, 0)
            row_max(1, 1)
            row_max(1, 2)
            row_max(1, 3)
            max_cols(1)
            save_values()
            k_low(3)
            row_max(2, 0)
            row_max(2, 1)
            row_max(2, 2)
            normalise(0)
            row_max(2, 3)
            max_cols(2)
            residual(0)
            row_max(3, 0)
            row_max(3, 1)
            row_max(3, 2)
            normalise(1)
            row_max(3, 3)
            max_cols(3)
            residual(1)
            normalise(2)
            normalise(3)
            residual(2)
            residual(3)

        @block.scalar
        def _(act):
            def h_high(b):
                t = b // 2
                act.wait_ge(gb_set, t + 1)
                nc.scalar.activation(h16[half(b), b, :], x_sb[half(b), t, :], ACT.Identity, bias=gb[half(b), t:t + 1],
                                     scale=ga[half(b), t:t + 1]).then_inc(hhi_set, 1)

            def q_high(b):
                act.wait_ge(q_done, b + 1)
                nc.scalar.activation(q_hi[:, b, :], ps_q[b % 2][:, 0:N], ACT.Identity, bias=b_h[:, 0:1]).then_inc(qhi_set, 1)

            def k_high(b):
                act.wait_ge(k_done, b + 1)
                if b == 0:
                    act.wait_ge(half_set, 1)
                    act.wait_ge(bh_set, 1)
                nc.scalar.activation(k_hi2[:, b, :], ps_k[:, 0:N], ACT.Identity, bias=kb[:, 0:1],
                                     scale=half_cols[:, 1:2]).then_inc(khi_set, 1)

            def k_second(b):
                if b == 0:
                    act.wait_ge(bh_set, 2)
                act.wait_ge(k1_set, b + 1)
                nc.scalar.activation(k_all[:, b, 1, :], ps_k[:, 0:N], ACT.Identity, bias=kb[:, 1:2],
                                     scale=half_cols[:, 0:1]).then_inc(k2_set, 1)

            def soft_exp(b, h):
                u = b * NH + h
                act.wait_ge(t_done, u + 1)
                if u >= RP:
                    act.wait_ge(pv_done, (u - RP) // NH + 1)
                nc.scalar.activation(probs[:, u % RP, :], t_bank(b, h), ACT.Exp, scale=SCALE
                                     ).then_inc(exp_done, 1)

            def q_low_max(b):
                act.wait_ge(m_done, b + 1)
                nc.scalar.activation(q_lom[:, b, :], ps_q[b % 2][:, 0:N], ACT.Identity, bias=b_h[:, 0:1]
                                     ).then_inc(qlom_set, 1)

            def save_out(b):
                act.wait_ge(pv_done, b + 1)
                nc.scalar.activation(o_sb[:, b, :], out_bank(b)[:, 0:N], ACT.Copy).then_inc(o_set, 1)

            def save_turned(b):
                act.wait_ge(ont_done, b + 1)
                nc.scalar.activation(ont_sb[:, b, :], out_bank(b)[0:C, N:2 * N], ACT.Copy).then_inc(ont_set, 1)

            act.wait_ge(wt_done, 1)
            nc.scalar.activation(w_part(0, 0), wt_qk, ACT.Copy)
            nc.scalar.activation(w_part(0, 1), wt_v, ACT.Copy).then_inc(whi_set, 1)
            h_high(0)
            h_high(1)
            k_high(0)
            q_high(0)
            k_second(0)
            h_high(2)
            k_high(1)
            h_high(3)
            k_second(1)
            q_high(1)
            k_high(2)
            q_low_max(0)
            k_second(2)
            q_high(2)
            soft_exp(0, 0)
            soft_exp(0, 1)
            k_high(3)
            soft_exp(0, 2)
            soft_exp(0, 3)
            q_low_max(1)
            k_second(3)
            save_out(0)
            soft_exp(1, 0)
            soft_exp(1, 1)
            soft_exp(1, 2)
            save_turned(0)
            q_high(3)
            q_low_max(2)
            soft_exp(1, 3)
            save_out(1)
            soft_exp(2, 0)
            soft_exp(2, 1)
            soft_exp(2, 2)
            save_turned(1)
            q_low_max(3)
            soft_exp(2, 3)
            soft_exp(3, 0)
            soft_exp(3, 1)
            soft_exp(3, 2)
            soft_exp(3, 3)
            save_out(2)
            save_out(3)
            save_turned(2)
            save_turned(3)


_INS = ['x', 'L0_conv_gn_w', 'L0_conv_gn_b', 'L0_conv_w_qkv', 'L0_conv_b_qkv', 'L0_conv_w_proj', 'L0_conv_b_proj']
_OUTS = [((4, 64, 16, 16), 'float32')]


def kernel(**inputs):
    import numpy as _np
    import concourse.bacc as _bacc
    from concourse import mybir as _mybir
    from concourse.bass_utils import run_bass_kernel_spmd as _run

    nc = _bacc.Bacc("TRN2", target_bir_lowering=False, num_devices=1)
    arrays, args = {}, []
    for name in _INS:
        a = _np.ascontiguousarray(inputs[name])
        arrays[f"in_{name}_dram"] = a
        args.append(nc.dram_tensor(f"in_{name}_dram", a.shape, _mybir.dt.from_np(a.dtype), kind="ExternalInput").ap())
    for i, (shape, dtype) in enumerate(_OUTS):
        dt = _mybir.dt.from_np(_np.dtype(dtype))
        args.append(nc.dram_tensor(f"out_{i}_dram", shape, dt, kind="ExternalOutput").ap())
    groupnorm_attention(nc, *args)
    r = _run(nc, [arrays], core_ids=[0])
    got = tuple(r.results[0][f"out_{i}_dram"] for i in range(len(_OUTS)))
    return got[0]
```
